# Optimizing a Trainium2 kernel written in Bass

```python
import numpy as np
import jax
import jax.numpy as jnp

def _softmax(x, axis=-1):
    return jax.nn.softmax(x, axis=axis)

def _gelu(x):
    return jax.nn.gelu(x, approximate=True)

def _silu(x):
    return jax.nn.silu(x)

def _sigmoid(x):
    return jax.nn.sigmoid(x)

def _layernorm(x, axis=-1, eps=1e-05):
    m = jnp.mean(x, axis=axis, keepdims=True)
    v = jnp.var(x, axis=axis, keepdims=True)
    return (x - m) / jnp.sqrt(v + eps)

def _scatter_add(tgt, idx, src, axis=0):
    return tgt.at[idx].add(src)

def _segment_sum(src, seg, n):
    return jax.ops.segment_sum(src, seg, n)
kernel_name = 'mk_lm_tower_d2_tok_ids1024_r4_b787ae'

def setup_inputs(seed: int=0):
    np.random.seed(seed)
    _w = jnp.asarray

    def _rec_inputs():
        import jax
        import jax.numpy as jnp
        _rk = jax.random.key(seed)
        x = jax.random.randint(jax.random.fold_in(_rk, 1), (16, 128), 0, 30521, jnp.int32)
        mask_BS_i1_0 = jnp.where(jnp.ones((16, 128), dtype=bool), 1, 0).astype(jnp.int32)
        itok_BS_0_511 = jax.random.randint(jax.random.fold_in(_rk, 22), (16, 128), 0, 128, jnp.int32)
        return (x, mask_BS_i1_0, itok_BS_0_511)
    x, mask_BS_i1_0, itok_BS_0_511 = _rec_inputs()

    def _L0_tok_setup():
        import jax, jax.numpy as jnp
        import numpy as np
        VOCAB = 30522
        HIDDEN = 256
        MAX_POS = 128
        TYPE_VOCAB = 2
        B, S = (32, 128)
        EPS = 1e-12
        key = jax.random.key(seed)
        ks = jax.random.split(key, 8)
        return {'input_ids': jax.random.randint(ks[0], (B, S), 0, VOCAB, dtype=jnp.int32), 'token_type_ids': jax.random.randint(ks[1], (B, S), 0, TYPE_VOCAB, dtype=jnp.int32), 'position_ids': jax.random.randint(ks[2], (B, S), 0, MAX_POS, dtype=jnp.int32), 'word_emb': jax.random.normal(ks[3], (VOCAB, HIDDEN), dtype=jnp.float32) * 0.02, 'pos_emb': jax.random.normal(ks[4], (MAX_POS, HIDDEN), dtype=jnp.float32) * 0.02, 'type_emb': jax.random.normal(ks[5], (TYPE_VOCAB, HIDDEN), dtype=jnp.float32) * 0.02, 'ln_gamma': jnp.ones((HIDDEN,), dtype=jnp.float32), 'ln_beta': jnp.zeros((HIDDEN,), dtype=jnp.float32)}
    _L0_tok_all = _L0_tok_setup()
    _L0_tok_in = {k: v for k, v in _L0_tok_all.items() if k in ('word_emb', 'pos_emb', 'type_emb', 'ln_gamma', 'ln_beta')}
    del _L0_tok_all

    def _L0_attn_setup():
        import jax, jax.numpy as jnp
        import numpy as np
        B, N, D, H = (4, 1024, 256, 16)
        DH = D // H
        M = int(DH * np.log(DH))
        EPS = 0.0001

        def softmax_kernel(t, proj, is_query):
            dn = t.shape[-1] ** (-0.25)
            ratio = proj.shape[0] ** (-0.5)
            td = jnp.einsum('bhnd,md->bhnm', t * dn, proj)
            diag = 0.5 * dn ** 2 * jnp.sum(t * t, axis=-1, keepdims=True)
            if is_query:
                mx = jnp.max(td, axis=-1, keepdims=True)
            else:
                mx = jnp.max(td, axis=(-1, -2), keepdims=True)
            return ratio * (jnp.exp(td - diag - mx) + EPS)
        key = jax.random.key(seed)
        ks = jax.random.split(key, 12)
        s = 0.02
        inp = {'x': jax.random.normal(ks[0], (B, N, D), jnp.float32), 'Wq': jax.random.normal(ks[1], (D, D), jnp.float32) * s, 'bq': jnp.zeros((D,), jnp.float32), 'Wk': jax.random.normal(ks[2], (D, D), jnp.float32) * s, 'bk': jnp.zeros((D,), jnp.float32), 'Wv': jax.random.normal(ks[3], (D, D), jnp.float32) * s, 'bv': jnp.zeros((D,), jnp.float32), 'Wo': jax.random.normal(ks[4], (D, D), jnp.float32) * s, 'bo': jnp.zeros((D,), jnp.float32), 'Wfc': jax.random.normal(ks[5], (D, D), jnp.float32) * s, 'bfc': jnp.zeros((D,), jnp.float32), 'proj': jax.random.normal(ks[6], (M, DH), jnp.float32)}
        return inp
    _L0_attn_all = _L0_attn_setup()
    _L0_attn_in = {k: v for k, v in _L0_attn_all.items() if k in ('Wq', 'bq', 'Wk', 'bk', 'Wv', 'bv', 'Wo', 'bo', 'Wfc', 'bfc', 'proj')}
    del _L0_attn_all

    def _L0_ffn_setup():
        import jax, jax.numpy as jnp
        import numpy as np
        IN_DIM, OUT_DIM, N_PROTO, RANK = (256, 256, 32, 16)
        key = jax.random.key(seed)
        ks = jax.random.split(key, 5)
        x = jax.random.normal(ks[0], (2, 1024, IN_DIM), dtype=jnp.float32)
        prototypes = jax.random.normal(ks[1], (N_PROTO, IN_DIM), dtype=jnp.float32) * 0.02
        B = jax.random.normal(ks[2], (N_PROTO, RANK, IN_DIM), dtype=jnp.float32) * 0.02
        A = jax.random.normal(ks[3], (N_PROTO, OUT_DIM, RANK), dtype=jnp.float32) * 0.02
        bias = jnp.zeros((N_PROTO, OUT_DIM), dtype=jnp.float32)
        temp = jnp.asarray(1.0, dtype=jnp.float32)
        return {'x': x, 'prototypes': prototypes, 'B': B, 'A': A, 'bias': bias, 'temp': temp}
    _L0_ffn_all = _L0_ffn_setup()
    _L0_ffn_in = {k: v for k, v in _L0_ffn_all.items() if k in ('prototypes', 'B', 'A', 'bias', 'temp')}
    del _L0_ffn_all

    def _L1_attn_setup():
        import jax, jax.numpy as jnp
        import numpy as np
        NUM_HEADS = 16
        THETA = 10000.0

        def _rotate_half(x):
            x = x.reshape(x.shape[:-1] + (-1, 2))
            x1, x2 = (x[..., 0], x[..., 1])
            return jnp.stack((-x2, x1), axis=-1).reshape(x.shape[:-2] + (-1,))

        def _rope(x):
            d_k = x.shape[-1]
            seq_len = x.shape[-2]
            inv_freq = 1.0 / THETA ** (jnp.arange(0, d_k, 2, dtype=jnp.float32) / d_k)
            pos = jnp.arange(seq_len, dtype=jnp.float32)
            theta = pos[:, None] * inv_freq[None, :]
            cos = jnp.repeat(jnp.cos(theta), 2, axis=-1)
            sin = jnp.repeat(jnp.sin(theta), 2, axis=-1)
            return x * cos + _rotate_half(x) * sin
        key = jax.random.key(seed)
        kx, kq, kk, kv, ko = jax.random.split(key, 5)
        B, S, D = (2, 512, 256)
        std = 1.0 / (2.0 * (2 * D) ** 0.5)
        return {'x': jax.random.normal(kx, (B, S, D), dtype=jnp.float32), 'Wq': jax.random.normal(kq, (D, D), dtype=jnp.float32) * std, 'Wk': jax.random.normal(kk, (D, D), dtype=jnp.float32) * std, 'Wv': jax.random.normal(kv, (D, D), dtype=jnp.float32) * std, 'Wo': jax.random.normal(ko, (D, D), dtype=jnp.float32) * std}
    _L1_attn_all = _L1_attn_setup()
    _L1_attn_in = {k: v for k, v in _L1_attn_all.items() if k in ('Wq', 'Wk', 'Wv', 'Wo')}
    del _L1_attn_all

    def _L1_ffn_setup():
        import jax, jax.numpy as jnp
        import numpy as np
        EPS = 1e-05

        def _quantize(W):
            gamma = jnp.mean(jnp.abs(W))
            return jnp.clip(jnp.round(W / (gamma + EPS)), -1.0, 1.0)
        key = jax.random.key(seed)
        k_x, k_w1, k_b1, k_w2, k_b2 = jax.random.split(key, 5)
        n_embd = 256
        d_ff = 4 * n_embd
        B, S = (4, 1024)
        bound1 = 1.0 / np.sqrt(n_embd)
        bound2 = 1.0 / np.sqrt(d_ff)
        x = jax.random.normal(k_x, (B, S, n_embd), dtype=jnp.float32)
        W1 = jax.random.uniform(k_w1, (d_ff, n_embd), jnp.float32, -bound1, bound1)
        b1 = jax.random.uniform(k_b1, (d_ff,), jnp.float32, -bound1, bound1)
        W2 = jax.random.uniform(k_w2, (n_embd, d_ff), jnp.float32, -bound2, bound2)
        b2 = jax.random.uniform(k_b2, (n_embd,), jnp.float32, -bound2, bound2)
        return {'x': x, 'W1': W1, 'b1': b1, 'W2': W2, 'b2': b2}
    _L1_ffn_all = _L1_ffn_setup()
    _L1_ffn_in = {k: v for k, v in _L1_ffn_all.items() if k in ('W1', 'b1', 'W2', 'b2')}
    del _L1_ffn_all
    return {'x': x, 'mask_BS_i1_0': mask_BS_i1_0, 'itok_BS_0_511': itok_BS_0_511, 'L0_tok_word_emb': _L0_tok_in['word_emb'], 'L0_tok_pos_emb': _L0_tok_in['pos_emb'], 'L0_tok_type_emb': _L0_tok_in['type_emb'], 'L0_tok_ln_gamma': _L0_tok_in['ln_gamma'], 'L0_tok_ln_beta': _L0_tok_in['ln_beta'], 'L0_attn_Wq': _L0_attn_in['Wq'], 'L0_attn_bq': _L0_attn_in['bq'], 'L0_attn_Wk': _L0_attn_in['Wk'], 'L0_attn_bk': _L0_attn_in['bk'], 'L0_attn_Wv': _L0_attn_in['Wv'], 'L0_attn_bv': _L0_attn_in['bv'], 'L0_attn_Wo': _L0_attn_in['Wo'], 'L0_attn_bo': _L0_attn_in['bo'], 'L0_attn_Wfc': _L0_attn_in['Wfc'], 'L0_attn_bfc': _L0_attn_in['bfc'], 'L0_attn_proj': _L0_attn_in['proj'], 'L0_ffn_prototypes': _L0_ffn_in['prototypes'], 'L0_ffn_B': _L0_ffn_in['B'], 'L0_ffn_A': _L0_ffn_in['A'], 'L0_ffn_bias': _L0_ffn_in['bias'], 'L0_ffn_temp': _L0_ffn_in['temp'], 'L1_attn_Wq': _L1_attn_in['Wq'], 'L1_attn_Wk': _L1_attn_in['Wk'], 'L1_attn_Wv': _L1_attn_in['Wv'], 'L1_attn_Wo': _L1_attn_in['Wo'], 'L1_ffn_W1': _L1_ffn_in['W1'], 'L1_ffn_b1': _L1_ffn_in['b1'], 'L1_ffn_W2': _L1_ffn_in['W2'], 'L1_ffn_b2': _L1_ffn_in['b2']}

def reference(x, mask_BS_i1_0, itok_BS_0_511, L0_tok_word_emb, L0_tok_pos_emb, L0_tok_type_emb, L0_tok_ln_gamma, L0_tok_ln_beta, L0_attn_Wq, L0_attn_bq, L0_attn_Wk, L0_attn_bk, L0_attn_Wv, L0_attn_bv, L0_attn_Wo, L0_attn_bo, L0_attn_Wfc, L0_attn_bfc, L0_attn_proj, L0_ffn_prototypes, L0_ffn_B, L0_ffn_A, L0_ffn_bias, L0_ffn_temp, L1_attn_Wq, L1_attn_Wk, L1_attn_Wv, L1_attn_Wo, L1_ffn_W1, L1_ffn_b1, L1_ffn_W2, L1_ffn_b2):
    import jax
    import jax.numpy as jnp

    def _L0_tok_ref(input_ids, token_type_ids, position_ids, word_emb, pos_emb, type_emb, ln_gamma, ln_beta):
        import jax, jax.numpy as jnp
        import numpy as np
        VOCAB = 30522
        HIDDEN = 256
        MAX_POS = 128
        TYPE_VOCAB = 2
        B, S = (32, 128)
        EPS = 1e-12
        x = word_emb[input_ids] + pos_emb[position_ids] + type_emb[token_type_ids]
        mean = jnp.mean(x, axis=-1, keepdims=True)
        var = jnp.mean(jnp.square(x - mean), axis=-1, keepdims=True)
        x_hat = (x - mean) * jax.lax.rsqrt(var + EPS)
        return x_hat * ln_gamma + ln_beta

    def _L0_attn_ref(x, Wq, bq, Wk, bk, Wv, bv, Wo, bo, Wfc, bfc, proj):
        import jax, jax.numpy as jnp
        import numpy as np
        B, N, D, H = (4, 1024, 256, 16)
        DH = D // H
        M = int(DH * np.log(DH))
        EPS = 0.0001

        def softmax_kernel(t, proj, is_query):
            dn = t.shape[-1] ** (-0.25)
            ratio = proj.shape[0] ** (-0.5)
            td = jnp.einsum('bhnd,md->bhnm', t * dn, proj)
            diag = 0.5 * dn ** 2 * jnp.sum(t * t, axis=-1, keepdims=True)
            if is_query:
                mx = jnp.max(td, axis=-1, keepdims=True)
            else:
                mx = jnp.max(td, axis=(-1, -2), keepdims=True)
            return ratio * (jnp.exp(td - diag - mx) + EPS)
        b, n, d = x.shape

        def heads(t):
            return t.reshape(b, n, H, DH).transpose(0, 2, 1, 3)
        q = heads(x @ Wq.T + bq)
        k = heads(x @ Wk.T + bk)
        v = heads(x @ Wv.T + bv)
        qp = softmax_kernel(q, proj, is_query=True)
        kp = softmax_kernel(k, proj, is_query=False)
        k_sum = jnp.sum(kp, axis=-2)
        d_inv = 1.0 / jnp.einsum('bhnm,bhm->bhn', qp, k_sum)
        context = jnp.einsum('bhnm,bhnd->bhmd', kp, v)
        out = jnp.einsum('bhmd,bhnm,bhn->bhnd', context, qp, d_inv)
        out = out.transpose(0, 2, 1, 3).reshape(b, n, d)
        h = out @ Wo.T + bo
        return jax.nn.relu(h @ Wfc.T + bfc)

    def _L0_ffn_ref(x, prototypes, B, A, bias, temp):
        import jax, jax.numpy as jnp
        import numpy as np
        IN_DIM, OUT_DIM, N_PROTO, RANK = (256, 256, 32, 16)
        lead = x.shape[:-1]
        xf = x.reshape(-1, IN_DIM)
        x2 = jnp.sum(xf * xf, axis=1, keepdims=True)
        p2 = jnp.sum(prototypes * prototypes, axis=1)
        d2 = x2 + p2[None, :] - 2.0 * (xf @ prototypes.T)
        dists = jnp.sqrt(jnp.maximum(d2, 0.0))
        t = jnp.maximum(jnp.abs(temp), 0.1)
        w = jax.nn.softmax(-dists / t, axis=1)
        topw, topi = jax.lax.top_k(w, 2)
        topw = topw / jnp.sum(topw, axis=1, keepdims=True)
        out = jnp.zeros((xf.shape[0], OUT_DIM), dtype=xf.dtype)
        for tslot in range(2):
            idx = topi[:, tslot]
            wt = topw[:, tslot:tslot + 1]
            h = jnp.einsum('nri,ni->nr', B[idx], xf)
            y = jnp.einsum('nor,nr->no', A[idx], h) + bias[idx]
            out = out + wt * y
        return out.reshape(*lead, OUT_DIM)

    def _L1_attn_ref(x, Wq, Wk, Wv, Wo):
        import jax, jax.numpy as jnp
        import numpy as np
        NUM_HEADS = 16
        THETA = 10000.0

        def _rotate_half(x):
            x = x.reshape(x.shape[:-1] + (-1, 2))
            x1, x2 = (x[..., 0], x[..., 1])
            return jnp.stack((-x2, x1), axis=-1).reshape(x.shape[:-2] + (-1,))

        def _rope(x):
            d_k = x.shape[-1]
            seq_len = x.shape[-2]
            inv_freq = 1.0 / THETA ** (jnp.arange(0, d_k, 2, dtype=jnp.float32) / d_k)
            pos = jnp.arange(seq_len, dtype=jnp.float32)
            theta = pos[:, None] * inv_freq[None, :]
            cos = jnp.repeat(jnp.cos(theta), 2, axis=-1)
            sin = jnp.repeat(jnp.sin(theta), 2, axis=-1)
            return x * cos + _rotate_half(x) * sin
        B, S, D = x.shape
        H = NUM_HEADS
        d_k = D // H

        def split_heads(t):
            return t.reshape(B, S, H, d_k).transpose(0, 2, 1, 3)
        Q = split_heads(x @ Wq)
        K = split_heads(x @ Wk)
        V = split_heads(x @ Wv)
        Q = _rope(Q)
        K = _rope(K)
        scores = jnp.einsum('bhqd,bhkd->bhqk', Q, K) / jnp.sqrt(jnp.float32(d_k))
        causal = jnp.tril(jnp.ones((S, S), dtype=bool))
        scores = jnp.where(causal[None, None], scores, -jnp.inf)
        attn = jax.nn.softmax(scores, axis=-1)
        out = jnp.einsum('bhqk,bhkd->bhqd', attn, V)
        out = out.transpose(0, 2, 1, 3).reshape(B, S, D)
        return out @ Wo

    def _L1_ffn_ref(x, W1, b1, W2, b2):
        import jax, jax.numpy as jnp
        import numpy as np
        EPS = 1e-05

        def _quantize(W):
            gamma = jnp.mean(jnp.abs(W))
            return jnp.clip(jnp.round(W / (gamma + EPS)), -1.0, 1.0)
        Wq1 = _quantize(W1)
        Wq2 = _quantize(W2)
        h = jax.nn.relu(jnp.einsum('bsd,fd->bsf', x, Wq1) + b1)
        out = jnp.einsum('bsf,df->bsd', h, Wq2) + b2
        return out
    h = _L0_tok_ref(x, mask_BS_i1_0, itok_BS_0_511, L0_tok_word_emb, L0_tok_pos_emb, L0_tok_type_emb, L0_tok_ln_gamma, L0_tok_ln_beta)
    h = h + _L0_attn_ref(_layernorm(h, axis=-1), L0_attn_Wq, L0_attn_bq, L0_attn_Wk, L0_attn_bk, L0_attn_Wv, L0_attn_bv, L0_attn_Wo, L0_attn_bo, L0_attn_Wfc, L0_attn_bfc, L0_attn_proj)
    h = h + _L0_ffn_ref(_layernorm(h, axis=-1), L0_ffn_prototypes, L0_ffn_B, L0_ffn_A, L0_ffn_bias, L0_ffn_temp)
    h = h + _L1_attn_ref(_layernorm(h, axis=-1), L1_attn_Wq, L1_attn_Wk, L1_attn_Wv, L1_attn_Wo)
    h = h + _L1_ffn_ref(_layernorm(h, axis=-1), L1_ffn_W1, L1_ffn_b1, L1_ffn_W2, L1_ffn_b2)
    return h

_drawn_inputs = setup_inputs


def setup_inputs(seed=0):
    import zlib

    import numpy as np

    out = dict(_drawn_inputs(seed))
    spreads = {'L0_tok_ln_gamma': (1.0, 0.2),
     'L0_tok_ln_beta': (0.0, 0.1),
     'L0_attn_bq': (0.0, 2.0),
     'L0_attn_bk': (0.0, 2.0),
     'L0_attn_bv': (0.0, 0.691),
     'L0_attn_bo': (0.0, 0.312),
     'L0_attn_bfc': (0.0, 0.1),
     'L0_ffn_bias': (0.0, 0.1)}
    factors = {'L0_attn_Wq': 64.0,
     'L0_attn_Wk': 64.0,
     'L0_attn_Wv': 4.039,
     'L0_attn_Wo': 4.243,
     'L0_attn_proj': 64.0,
     'L0_ffn_B': 3.389,
     'L0_ffn_A': 3.407,
     'L1_attn_Wq': 8.0,
     'L1_attn_Wk': 8.0,
     'L1_ffn_b1': 23.026,
     'L1_ffn_b2': 64.0}
    for name, (base, spread) in spreads.items():
        noise = np.random.default_rng([zlib.crc32(name.encode()), seed]).standard_normal(out[name].shape)
        drawn = base * np.exp(spread * noise) if base else spread * noise
        out[name] = jnp.asarray(drawn.astype(out[name].dtype))
    for name, factor in factors.items():
        out[name] = (out[name] * factor).astype(out[name].dtype)
    return out
```

```python
from contextlib import ExitStack

import numpy as np

import concourse.bass as bass
from concourse import mybir

ALU = mybir.AluOpType
ACT = mybir.ActivationFunctionType
F32 = mybir.dt.float32
F16 = mybir.dt.float16
BF16 = mybir.dt.bfloat16
I32 = mybir.dt.int32
U32 = mybir.dt.uint32
AX_X = mybir.AxisListType.X

P = 128
D = 256
KC = D // P
TILES = 16
H = 16
DH = D // H
M = 44
HP = H // 2
MP = 2 * M
VA = DH + 1
PROTO = 32
RANK = 16
R2 = PROTO * RANK
F1 = 1024
FC = F1 // P
VOCAB, POS, TYPES = 30522, 128, 2
FEATURE_EPS = 1e-4
EMB_EPS, LN_EPS, QUANT_EPS = 1e-12, 1e-5, 1e-5
HIDDEN_SCORE = -1e30
SLOT = 32

SKEW = {"E": -1, "P": 0, "F": 1, "R": 2, "M": 3}
FIRST_STEP, LAST_STEP = -1, TILES - 1 + SKEW["M"]
LOOP_FROM, LOOP_TO = SKEW["M"] + 1, TILES - 2


class Step:

    def __init__(self, i):
        self.i = i
        self.static = isinstance(i, int)

    def has(self, stage):
        return not self.static or 0 <= self.i - SKEW[stage] < TILES

    def tile(self, stage):
        return self.i - SKEW[stage]

    def before(self, stage):
        t = self.i - SKEW[stage]
        return min(max(t, 0), TILES) if self.static else t

    def after(self, stage):
        return self.before(stage) + (1 if self.has(stage) else 0)

    def next_gather(self):
        return not self.static or 0 <= self.i + 2 < TILES


def wait(eng, sem, count):
    if not (isinstance(count, int) and count <= 0):
        eng.wait_ge(sem, count)


def program(nc, A, out):
    with ExitStack() as ctx:
        def sb(name, shape, dt=F32):
            return ctx.enter_context(nc.sbuf_tensor(name, shape, dt))

        def sem(name):
            return ctx.enter_context(nc.semaphore(name))

        PS = ctx.enter_context(nc.psum_tensor("PS", [P, 8, 512], F32))

        ids = sb("ids", [P, 3, TILES], I32)
        ids_neg = sb("ids_neg", [P, 3, TILES], I32)
        idx = sb("idx", [P, 3], I32)
        gamma = sb("gamma", [P, D])
        beta = sb("beta", [P, D])
        wqkT = sb("wqkT", [P, KC, 2 * D])
        wvT = sb("wvT", [P, KC, D])
        wo = sb("wo", [P, KC, D])
        wfcT = sb("wfcT", [P, KC, D])
        wof = sb("wof", [P, KC, D])
        bqk = sb("bqk", [P, 4])
        bv = sb("bv", [P, D])
        bo = sb("bo", [P, KC])
        bfc = sb("bfc", [P, D])
        bof = sb("bof", [P, D])
        proj = sb("proj", [P, 8 * M])
        half_sq = sb("half_sq", [P, KC, H])
        ones = sb("ones", [P, P])
        ident = sb("ident", [P, P])
        ident_b = sb("ident_b", [P, P], BF16)
        pair_mask = sb("pair_mask", [MP, HP, 2 * VA])
        protoT = sb("protoT", [P, KC, PROTO])
        protoT2 = sb("protoT2", [P, KC, PROTO])
        proto_sq = sb("proto_sq", [P, KC, PROTO])
        p2 = sb("p2", [1, PROTO])
        fbT = sb("fbT", [P, KC, R2])
        faT = sb("faT", [P, R2 // P, D])
        fbias = sb("fbias", [PROTO, D])
        temp = sb("temp", [P, 4])
        iota_i = sb("iota_i", [P, PROTO], I32)
        iota = sb("iota", [P, PROTO])
        consts = sb("consts", [P, 4])
        halves = sb("halves", [P, PROTO])
        rope_cos = sb("rope_cos", [P, 2 * D])
        rope_sin = sb("rope_sin", [P, 2 * D])
        rwqk = sb("rwqk", [P, KC, 2 * D])
        rwv = sb("rwv", [P, KC, D])
        rwo = sb("rwo", [P, KC, D])
        mask_f = sb("mask_f", [P, 2, P])
        mask_qk = sb("mask_qk", [P, 4, P], BF16)
        mask_kq = sb("mask_kq", [P, 4, P], BF16)
        w1 = sb("w1", [P, KC * F1])
        w2 = sb("w2", [P, FC * D])
        wpos = sb("wpos", [P, KC * F1])
        wneg = sb("wneg", [P, KC * F1])
        w1q = sb("w1q", [P, KC, F1], F16)
        w2q = sb("w2q", [P, FC, D])
        absum = sb("absum", [P, 2])
        thr = sb("thr", [P, 4])
        b1 = sb("b1", [P, FC])
        b2 = sb("b2", [P, D])

        hres = sb("hres", [P, TILES, D])

        def h_of(t):
            return hres[:, bass.ds(t, 1), :].rearrange("p a n -> p (a n)")

        emb = sb("emb", [P, 3, D])
        esum1 = sb("esum1", [P, D])
        esum = sb("esum", [P, D])
        ehat = sb("ehat", [P, D])
        escaled = sb("escaled", [P, D])

        LNS = ("E", "P", "F", "R", "M")
        stats = {x: sb(f"stats{x}", [P, 6]) for x in LNS}
        mv = {x: sb(f"mv{x}", [P, 2]) for x in LNS}
        rstd = {x: sb(f"rstd{x}", [P, 2]) for x in LNS}
        xn = {x: sb(f"xn{x}", [P, D]) for x in "PFRM"}
        xT = {x: sb(f"xT{x}", [P, KC, P]) for x in "PFR"}

        qkT = sb("qkT", [P, 4, P])
        sqT = sb("sqT", [P, 4, P])
        va = sb("va", [P, H, VA])
        kmx = sb("kmx", [P, H])
        kmx_row = sb("kmx_row", [H, 1])
        kdiag = sb("kdiag", [H, H])
        kb = sb("kb", [P, 2 * H])
        kd = sb("kd", [P, H * M])
        ke = sb("ke", [P, H * M])
        kp = sb("kp", [P, H * M])
        ctxt = sb("ctxt", [MP, HP, 2 * VA])
        qmx = sb("qmx", [P, H])
        qb = sb("qb", [P, H])
        qd = sb("qd", [P, H * M])
        qe = sb("qe", [P, H * M])
        qp = sb("qp", [MP, HP, P])
        oden = sb("oden", [P, H])
        onorm = sb("onorm", [P, D])
        oT = sb("oT", [P, KC, P])
        ofb = sb("ofb", [P, D])

        xsq = sb("xsq", [P, D])
        x2 = sb("x2", [P, 1])
        d2 = sb("d2", [P, PROTO])
        dist = sb("dist", [P, PROTO])
        ndist = sb("ndist", [P, PROTO])
        top = sb("top", [P, 8])
        topi = sb("topi", [P, 8], U32)
        topf = sb("topf", [P, 2])
        gap = sb("gap", [P, 1])
        second = sb("second", [P, 1])
        wsum = sb("wsum", [P, 2])
        gate1 = sb("gate1", [P, PROTO])
        hg = sb("hg", [P, R2 + PROTO])
        hgT = sb("hgT", [P, R2 // P, P])
        gT = sb("gT", [PROTO, P])

        rc = sb("rc", [P, 2 * D])
        rs = sb("rs", [P, 2 * D])
        rpad = sb("rpad", [P, 2 * H, SLOT])
        rva = sb("rva", [P, H, VA])
        rT = sb("rT", [P, 8, P])
        rqT = sb("rqT", [P, 4, P])
        pT = sb("pT", [P, 4, 4, P])
        rden = sb("rden", [P, H])
        rout = sb("rout", [P, D])
        roT = sb("roT", [P, KC, P])

        xhi = sb("xhi", [P, KC, P], F16)
        xlo = sb("xlo", [P, KC, P], F16)
        mh = sb("mh", [P, FC, P])
        hb = sb("hb", [P, D])
        outb = sb("outb", [P, D])

        ids_in = sem("ids_in"); load = {x: sem(f"weights_in_{x}") for x in "EPFRM"}
        proj_zero = sem("proj_zero"); proj_in = sem("proj_in")
        gathered = sem("gathered"); ids_ok = sem("ids_ok"); idx_ok = sem("idx_ok")
        g_const = sem("g_const"); v_const = sem("v_const"); s_const = sem("s_const")
        wof_ps = sem("wof_ps"); wof_ok = sem("wof_ok"); p2_ps = sem("p2_ps"); p2_ok = sem("p2_ok")
        tern_abs = sem("tern_abs"); tern_ps = sem("tern_ps"); tern = sem("tern")
        v_held = sem("v_held"); g_held = sem("g_held")
        ln_v = {x: sem(f"ln_v_{x}") for x in LNS}; ln_g = {x: sem(f"ln_g_{x}") for x in LNS}
        e_sum = sem("e_sum"); e_out = sem("e_out")
        xT_ps = {x: sem(f"xT_ps_{x}") for x in "PFRM"}; xT_ok = {x: sem(f"xT_ok_{x}") for x in "PFRM"}
        qk_ps = sem("qk_ps"); qk_ok = sem("qk_ok"); sq_ok = sem("sq_ok")
        v_ps = sem("v_ps"); v_ok = sem("v_ok")
        tdk_ps = sem("tdk_ps"); kmx_ok = sem("kmx_ok"); kmxT_ps = sem("kmxT_ps"); kdiag_ok = sem("kdiag_ok")
        kb_ps = sem("kb_ps"); kb_ok = sem("kb_ok"); kd_ok = sem("kd_ok"); ke_ok = sem("ke_ok"); kp_ok = sem("kp_ok")
        ctx_ps = sem("ctx_ps"); ctx_ok = sem("ctx_ok")
        tdq_ps = sem("tdq_ps"); qb_ok = sem("qb_ok"); qd_ok = sem("qd_ok"); qe_ok = sem("qe_ok")
        qp_ps = sem("qp_ps"); qp_ok = sem("qp_ok")
        o_ps = sem("o_ps"); o_ok = sem("o_ok"); oT_ps = sem("oT_ps"); oT_ok = sem("oT_ok")
        of_ps = sem("of_ps"); hP_ok = sem("hP_ok")
        x2_ok = sem("x2_ok"); fh_ps = sem("fh_ps"); proto_ps = sem("proto_ps"); d2_ok = sem("d2_ok"); dist_ok = sem("dist_ok")
        gap_ok = sem("gap_ok"); second_ok = sem("second_ok"); gate_ok = sem("gate_ok"); hg_ok = sem("hg_ok")
        hgT_ps = sem("hgT_ps"); hgT_ok = sem("hgT_ok"); y_ps = sem("y_ps"); hF_ok = sem("hF_ok")
        rqk_ps = sem("rqk_ps"); rope_ok = sem("rope_ok"); rot_ok = sem("rot_ok")
        rv_ps = sem("rv_ps"); rv_ok = sem("rv_ok"); rT_ps = sem("rT_ps"); rT_ok = sem("rT_ok")
        s1_ps = sem("s1_ps"); rmax_ok = sem("rmax_ok"); rqT_ps = sem("rqT_ps"); rqT_ok = sem("rqT_ok")
        s2_ps = sem("s2_ps"); pT_ok = sem("pT_ok"); pv_ps = sem("pv_ps"); ro_ok = sem("ro_ok")
        roT_ps = sem("roT_ps"); roT_ok = sem("roT_ok"); wo_ps = sem("wo_ps"); hR_ok = sem("hR_ok")
        xlo_ok = sem("xlo_ok"); m_ps = sem("m_ps"); mh_ok = sem("mh_ok"); hb_ok = sem("hb_ok")
        y2_ps = sem("y2_ps"); out_ok = sem("out_ok"); stored = sem("stored")

        N_LOAD = {"E": 2, "P": 8, "F": 5, "R": 5, "M": 4}
        G_CONST, V_CONST = 14, 9

        block = ctx.enter_context(nc.Block())

        @block.sync
        def _(sp):
            def get(x, dst, src):
                sp.dma_start(dst, src).then_inc(load[x], 16)

            sp.dma_start(ids[:, :, :], A["ids"]).then_inc(ids_in, 16)
            get("E", gamma[:, :], A["gamma"].partition_broadcast(P))
            get("E", beta[:, :], A["beta"].partition_broadcast(P))
            get("P", wqkT[:, :, :], A["wqkT"].rearrange("(c p) n -> p c n", p=P))
            get("P", wvT[:, :, :], A["wvT"].rearrange("(c p) n -> p c n", p=P))
            get("P", bqk[:, :], A["bqk"])
            get("P", bv[:, :], A["bv"].partition_broadcast(P))
            get("P", wo[:, :, :], A["wo"].rearrange("(c p) n -> p c n", p=P))
            get("P", wfcT[:, :, :], A["wfcT"].rearrange("(c p) n -> p c n", p=P))
            get("P", bo[:, :], A["bo"])
            get("P", bfc[:, :], A["bfc"].partition_broadcast(P))
            sp.wait_ge(proj_zero, 1)
            for j in range(8):
                sp.dma_start(proj[DH * j:DH * (j + 1), M * j:M * (j + 1)], A["projT"]).then_inc(proj_in, 16)
            get("F", protoT[:, :, :], A["protoT"].rearrange("(c p) n -> p c n", p=P))
            get("F", fbT[:, :, :], A["fbT"].rearrange("(c p) n -> p c n", p=P))
            get("F", faT[:, :, :], A["faT"].rearrange("(c p) n -> p c n", p=P))
            get("F", fbias[:, :], A["fbias"])
            get("F", temp[:, 0:1], A["temp"].partition_broadcast(P))
            get("R", rwqk[:, :, :], A["rwqk"].rearrange("(c p) n -> p c n", p=P))
            get("R", rwv[:, :, :], A["rwv"].rearrange("(c p) n -> p c n", p=P))
            get("R", rwo[:, :, :], A["rwo"].rearrange("(c p) n -> p c n", p=P))
            get("R", rope_cos[:, :], A["rope_cos"])
            get("R", rope_sin[:, :], A["rope_sin"])
            get("M", w1[:, :].rearrange("p (c n) -> p c n", c=KC), A["w1T"].rearrange("(c p) n -> p c n", p=P))
            get("M", w2[:, :].rearrange("p (c n) -> p c n", c=FC), A["w2T"].rearrange("(c p) n -> p c n", p=P))
            get("M", b1[:, :], A["b1"])
            get("M", b2[:, :], A["b2"].partition_broadcast(P))
            with sp.Fori(0, TILES) as t:
                sp.wait_ge(out_ok, t + 1)
                sp.dma_start(out[bass.ds(t, 1), :, :].rearrange("a p n -> p (a n)"), outb[:, :]).then_inc(stored, 16)
            sp.wait_ge(stored, 16 * TILES)

        @block.gpsimd
        def _(g):
            def held(sem_, count):
                wait(g, sem_, count)
                g.sem_inc(g_held, 1)

            tables = (A["word"], A["pos"], A["type"])

            def gather(t):
                held(idx_ok, t)
                g.tensor_copy(idx[:, :].unsqueeze(2), ids[:, :, bass.ds(t, 1)]).then_inc(idx_ok, 1)
                held(idx_ok, t + 1)
                for k in range(3):
                    g.indirect_dma_start(emb[:, k, :], None, tables[k],
                                         bass.IndirectOffsetOnAxis(idx[:, k:k + 1], 0)).then_inc(gathered, 16)

            g.memset(proj[:, :], 0.0).then_inc(proj_zero, 1)
            g.wait_ge(ids_ok, 3)
            gather(0)
            n = 0
            for t_, v_ in ((consts[:, 0:1], -0.5), (consts[:, 1:2], EMB_EPS), (consts[:, 2:3], LN_EPS),
                           (halves[:, :], 0.5), (ones[:, :], 1.0), (ident[:, :], 0.0),
                           (half_sq[:, :, :], 0.125), (mask_f[:, :, :], 0.0), (pair_mask[:, :, :], 1.0)):
                g.memset(t_, v_).then_inc(g_const, 1)
            g.iota(iota_i[:, :], pattern=[[1, PROTO]], base=0, channel_multiplier=0).then_inc(g_const, 1)
            g.wait_ge(g_const, 10)
            g.affine_select(out=ident[:, :], in_=ident[:, :], compare_op=ALU.not_equal, fill=1.0, base=0,
                            pattern=[[-1, P]], channel_multiplier=1).then_inc(g_const, 1)
            g.affine_select(out=half_sq[:, :, :], in_=half_sq[:, :, :], compare_op=ALU.is_ge, fill=0.0, base=0,
                            pattern=[[P, KC], [-DH, H]], channel_multiplier=1).then_inc(g_const, 1)
            g.affine_select(out=mask_f[:, 0, :], in_=mask_f[:, 0, :], compare_op=ALU.is_ge, fill=HIDDEN_SCORE,
                            base=0, pattern=[[-1, P]], channel_multiplier=1).then_inc(g_const, 1)
            g.affine_select(out=mask_f[:, 1, :], in_=mask_f[:, 1, :], compare_op=ALU.is_ge, fill=HIDDEN_SCORE,
                            base=0, pattern=[[1, P]], channel_multiplier=-1).then_inc(g_const, 1)
            g.affine_select(out=pair_mask[:, :, 0:VA], in_=pair_mask[:, :, 0:VA], compare_op=ALU.is_ge, fill=0.0,
                            base=M - 1, pattern=[[0, HP], [0, VA]], channel_multiplier=-1).then_inc(g_const, 1)
            g.affine_select(out=pair_mask[:, :, VA:], in_=pair_mask[:, :, VA:], compare_op=ALU.is_ge, fill=0.0,
                            base=-M, pattern=[[0, HP], [0, VA]], channel_multiplier=1).then_inc(g_const, 1)
            g.wait_ge(g_const, 16)
            g.affine_select(out=half_sq[:, :, :], in_=half_sq[:, :, :], compare_op=ALU.is_ge, fill=0.0, base=DH - 1,
                            pattern=[[-P, KC], [DH, H]], channel_multiplier=-1).then_inc(g_const, 1)
            g.wait_ge(load["E"], 16 * N_LOAD["E"])

            def ln_power(x, t, eps_col):
                wait(g, ln_v[x], 3 * t + 2)
                g.tensor_tensor(rstd[x][:, 0:1], mv[x][:, 1:2], consts[:, eps_col:eps_col + 1], ALU.add)\
                    .then_inc(ln_g[x], 1)
                wait(g, ln_g[x], 2 * t + 1)
                g.tensor_tensor(rstd[x][:, 1:2], rstd[x][:, 0:1], consts[:, 0:1], ALU.pow).then_inc(ln_g[x], 1)

            def step(s):
                if s.has("M"):
                    t = s.tile("M")
                    if s.static and t == 0:
                        g.wait_ge(load["M"], 16 * N_LOAD["M"])
                    wait(g, hR_ok, t + 1)
                    wait(g, out_ok, t)
                    g.tensor_tensor(hb[:, :], h_of(t), b2[:, :], ALU.add).then_inc(hb_ok, 1)
                if s.has("R"):
                    t = s.tile("R")
                    wait(g, rope_ok, 3 * t + 3)
                    wait(g, rqT_ps, t)
                    g.tensor_tensor(rpad[:, :, 0:DH], rc[:, :].rearrange("p (h d) -> p h d", d=DH),
                                    rs[:, :].rearrange("p (h d) -> p h d", d=DH), ALU.add).then_inc(rot_ok, 1)
                if s.has("F"):
                    t = s.tile("F")
                    wait(g, d2_ok, t + 1)
                    g.tensor_tensor(dist[:, :], d2[:, :], halves[:, :], ALU.pow).then_inc(dist_ok, 1)
                if s.has("E"):
                    t = s.tile("E")
                    wait(g, gathered, 48 * t + 48)
                    g.tensor_tensor(esum1[:, :], emb[:, 0, :], emb[:, 1, :], ALU.add).then_inc(e_sum, 1)
                    wait(g, e_sum, 2 * t + 1)
                    g.tensor_tensor(esum[:, :], esum1[:, :], emb[:, 2, :], ALU.add).then_inc(e_sum, 1)
                    if s.next_gather():
                        wait(g, e_sum, 2 * t + 2)
                        gather(t + 1)
                    ln_power("E", t, 1)
                    wait(g, ln_v["E"], 3 * t + 3)
                    g.tensor_tensor(escaled[:, :], ehat[:, :], gamma[:, :], ALU.mult).then_inc(e_out, 1)
                    wait(g, e_out, 2 * t + 1)
                    g.tensor_tensor(h_of(t), escaled[:, :], beta[:, :], ALU.add).then_inc(e_out, 1)
                    ln_power("P", t, 2)
                if s.has("F"):
                    ln_power("R", s.tile("F"), 2)
                if s.has("P"):
                    ln_power("F", s.tile("P"), 2)
                if s.has("R"):
                    ln_power("M", s.tile("R"), 2)

            for i in range(FIRST_STEP, LOOP_FROM):
                step(Step(i))
            with g.Fori(LOOP_FROM, LOOP_TO) as i:
                step(Step(i))
            for i in range(LOOP_TO, LAST_STEP + 1):
                step(Step(i))

        @block.vector
        def _(v):
            def held(sem_, count):
                wait(v, sem_, count)
                v.sem_inc(v_held, 1)

            def bc(ap, shape):
                return ap.to_broadcast(shape)

            v.wait_ge(ids_in, 16)
            for k, n in enumerate((VOCAB, POS, TYPES)):
                v.tensor_scalar(ids_neg[:, k, :], ids[:, k, :], 0.0, float(n), ALU.is_lt, ALU.mult).then_inc(v_const, 1)
            for k in range(3):
                v.wait_ge(v_const, k + 1)
                v.tensor_tensor(ids[:, k, :], ids[:, k, :], ids_neg[:, k, :], ALU.add).then_inc(v_const, 1)
            for k, n in enumerate((VOCAB, POS, TYPES)):
                v.wait_ge(v_const, 4 + k)
                v.tensor_scalar(ids[:, k, :], ids[:, k, :], 0.0, float(n - 1), ALU.max, ALU.min).then_inc(ids_ok, 1)

            def norm_stats(x, t, src, sem_, count):
                held(sem_, count)
                v.bn_stats(stats[x][:, :], src).then_inc(ln_v[x], 1)
                held(ln_v[x], 3 * t + 1)
                v.bn_aggr(mv[x][:, :], stats[x][:, :]).then_inc(ln_v[x], 1)

            def norm_apply(x, t, src, dst):
                wait(v, ln_g[x], 2 * t + 2)
                v.tensor_scalar(dst, src, mv[x][:, 0:1], rstd[x][:, 1:2], ALU.subtract, ALU.mult)\
                    .then_inc(ln_v[x], 1)

            def td(bank):
                return PS[:, bank:bank + 2, 0:8 * M].rearrange("p b (h m) -> p b h m", m=M)

            def heads(tile_):
                return tile_[:, :].rearrange("p (b h m) -> p b h m", b=2, m=M)

            def per_head(ap):
                return bc(ap.rearrange("p (b h) -> p b h", b=2).unsqueeze(3), [P, 2, 8, M])

            def setup_p():
                v.wait_ge(proj_in, 16 * 8)
                v.tensor_scalar(proj[:, :], proj[:, :], 0.5, None, ALU.mult).then_inc(s_const, 1)
                v.memset(va[:, :, :], 1.0).then_inc(s_const, 1)
                v.wait_ge(s_const, 2)
                v.wait_ge(wof_ps, 3)
                v.tensor_copy(wof[:, :, :], PS[:, 4:6, 0:D]).then_inc(wof_ok, 1)
                v.wait_ge(load["P"], 16 * N_LOAD["P"])
                v.tensor_tensor(bof[:, :], PS[:, 6, 0:D], bfc[:, :], ALU.add).then_inc(wof_ok, 1)
                v.wait_ge(wof_ok, 2)

            def setup_f():
                v.wait_ge(load["F"], 16 * N_LOAD["F"])
                v.tensor_tensor(proto_sq[:, :, :], protoT[:, :, :], protoT[:, :, :], ALU.mult).then_inc(p2_ok, 1)
                v.tensor_scalar(protoT2[:, :, :], protoT[:, :, :], -2.0, None, ALU.mult).then_inc(p2_ok, 1)
                v.wait_ge(g_const, 17)
                v.tensor_copy(iota[:, :], iota_i[:, :]).then_inc(p2_ok, 1)
                v.tensor_scalar(temp[:, 1:2], temp[:, 0:1], -1.0, None, ALU.mult).then_inc(p2_ok, 1)
                v.wait_ge(p2_ok, 4)
                v.tensor_tensor(temp[:, 2:3], temp[:, 0:1], temp[:, 1:2], ALU.max).then_inc(p2_ok, 1)
                v.wait_ge(p2_ok, 5)
                v.tensor_scalar(temp[:, 3:4], temp[:, 2:3], 0.1, -1.0, ALU.max, ALU.mult).then_inc(p2_ok, 1)
                v.wait_ge(p2_ok, 6)
                v.reciprocal(temp[:, 2:3], temp[:, 3:4]).then_inc(p2_ok, 1)
                v.wait_ge(p2_ok, 7)
                v.wait_ge(p2_ps, 1)
                v.tensor_copy(p2[:, :], PS[0:1, 6, 0:PROTO]).then_inc(p2_ok, 1)

            def setup_rm():
                v.memset(rpad[:, :, :], 0.0).then_inc(tern_abs, 1)
                v.memset(rva[:, :, :], 1.0).then_inc(tern_abs, 1)
                v.wait_ge(tern_abs, 2)
                v.memset(rpad[:, H:2 * H, DH:DH + 1], 1.0).then_inc(tern_abs, 1)
                v.wait_ge(load["R"], 16 * N_LOAD["R"])
                v.tensor_scalar(rope_cos[:, 0:D], rope_cos[:, 0:D], 0.25, None, ALU.mult).then_inc(tern_abs, 1)
                v.tensor_scalar(rope_sin[:, 0:D], rope_sin[:, 0:D], 0.25, None, ALU.mult).then_inc(tern_abs, 1)
                v.tensor_copy(ident_b[:, :], ident[:, :]).then_inc(tern_abs, 1)
                v.tensor_copy(mask_qk[:, :, :], bc(mask_f[:, 0:1, :], [P, 4, P])).then_inc(tern_abs, 1)
                v.tensor_copy(mask_kq[:, :, :], bc(mask_f[:, 1:2, :], [P, 4, P])).then_inc(tern_abs, 1)
                v.wait_ge(load["M"], 16 * N_LOAD["M"])
                v.tensor_reduce(absum[:, 0:1], w1[:, :], AX_X, ALU.add, apply_absolute_value=True).then_inc(tern_abs, 1)
                v.tensor_reduce(absum[:, 1:2], w2[:, :], AX_X, ALU.add, apply_absolute_value=True).then_inc(tern_abs, 1)
                v.wait_ge(tern_ps, 1)
                v.tensor_scalar(thr[:, 0:2], PS[:, 6, 0:2], 1.0 / (D * F1), QUANT_EPS, ALU.mult, ALU.add)\
                    .then_inc(tern, 1)
                v.wait_ge(tern, 1)
                v.tensor_scalar(thr[:, 2:4], thr[:, 0:2], -0.5, None, ALU.mult).then_inc(tern, 1)
                v.wait_ge(tern, 2)
                v.tensor_scalar(thr[:, 0:2], thr[:, 0:2], 0.5, None, ALU.mult).then_inc(tern, 1)
                v.wait_ge(tern, 3)
                n = 3
                for k, (w, dst) in enumerate(((w1, w1q[:, :, :].rearrange("p c n -> p (c n)")),
                                              (w2, w2q[:, :, :].rearrange("p c n -> p (c n)")))):
                    v.tensor_scalar(wpos[:, :], w[:, :], thr[:, k:k + 1], None, ALU.is_gt).then_inc(tern, 1)
                    v.tensor_scalar(wneg[:, :], w[:, :], thr[:, 2 + k:3 + k], None, ALU.is_lt).then_inc(tern, 1)
                    v.wait_ge(tern, n + 2)
                    v.tensor_tensor(dst, wpos[:, :], wneg[:, :], ALU.subtract).then_inc(tern, 1)
                    n += 3
                    v.wait_ge(tern, n)

            def step(s):
                if s.has("R"):
                    t = s.tile("R")
                    wait(v, rqk_ps, t + 1)
                    wait(v, rot_ok, t)
                    v.tensor_tensor(rc[:, :], PS[:, 4, :], rope_cos[:, :], ALU.mult).then_inc(rope_ok, 1)
                    x = PS[:, 4, :].rearrange("p (n two) -> p n two", two=2)
                    y = rs[:, :].rearrange("p (n two) -> p n two", two=2)
                    z = rope_sin[:, :].rearrange("p (n two) -> p n two", two=2)
                    v.tensor_tensor(y[:, :, 0], x[:, :, 1], z[:, :, 0], ALU.mult).then_inc(rope_ok, 1)
                    v.tensor_tensor(y[:, :, 1], x[:, :, 0], z[:, :, 1], ALU.mult).then_inc(rope_ok, 1)
                if s.has("P"):
                    t = s.tile("P")
                    wait(v, qk_ps, t + 1)
                    wait(v, sq_ok, t)
                    wait(v, tdq_ps, t)
                    v.tensor_tensor(qkT[:, :, :], PS[:, 7, :].rearrange("p (c n) -> p c n", c=4),
                                    bc(bqk[:, :].unsqueeze(2), [P, 4, P]), ALU.add).then_inc(qk_ok, 1)
                if s.has("M"):
                    t = s.tile("M")
                    wait(v, xT_ok["M"], t + 1)
                    wait(v, m_ps, t)
                    v.tensor_tensor(xlo[:, :, :], PS[:, 5, 0:D].rearrange("p (c n) -> p c n", c=KC), xhi[:, :, :],
                                    ALU.subtract).then_inc(xlo_ok, 1)
                if s.has("P"):
                    t = s.tile("P")
                    wait(v, v_ps, t + 1)
                    wait(v, ctx_ps, t)
                    v.tensor_tensor(va[:, :, 0:DH], PS[:, 7, 0:D].rearrange("p (h d) -> p h d", d=DH),
                                    bv[:, :].rearrange("p (h d) -> p h d", d=DH), ALU.add).then_inc(v_ok, 1)
                    wait(v, tdk_ps, t + 1)
                    v.tensor_reduce(kmx[:, :].rearrange("p (b h) -> p b h", b=2), td(4), AX_X, ALU.max)\
                        .then_inc(kmx_ok, 1)
                if s.has("P"):
                    t = s.tile("P")
                    wait(v, kmxT_ps, t + 1)
                    v.tensor_reduce(kmx_row[:, :], PS[0:H, 6, 0:P], AX_X, ALU.max).then_inc(kdiag_ok, 1)
                    wait(v, kdiag_ok, 2 * t + 1)
                    v.tensor_scalar(kdiag[:, :], ident[0:H, 0:H], kmx_row[:, 0:1], None, ALU.mult)\
                        .then_inc(kdiag_ok, 1)
                if s.has("F"):
                    t = s.tile("F")
                    wait(v, proto_ps, t + 1)
                    wait(v, x2_ok, t + 1)
                    v.tensor_scalar(d2[:, :], PS[:, 6, 0:PROTO], x2[:, 0:1], 0.0, ALU.add, ALU.max).then_inc(d2_ok, 1)
                if s.has("R"):
                    t = s.tile("R")
                    wait(v, s1_ps, t + 1)
                    v.tensor_reduce(rpad[:, 0:H, DH].rearrange("p (c j) -> p j c", j=4),
                                    PS[:, 0:4, :].rearrange("p j (c k) -> p j c k", c=4), AX_X, ALU.max,
                                    negate=True).then_inc(rmax_ok, 1)
                if s.has("P"):
                    t = s.tile("P")
                    wait(v, kb_ok, t + 1)
                    wait(v, ke_ok, t)
                    v.tensor_tensor(heads(kd), td(4), per_head(kb[:, 0:H]), ALU.subtract).then_inc(kd_ok, 1)
                if s.has("F"):
                    t = s.tile("F")
                    wait(v, dist_ok, t + 1)
                    v.tensor_scalar(ndist[:, :], dist[:, :], temp[:, 2:3], None, ALU.mult).then_inc(gap_ok, 1)
                    held(gap_ok, 5 * t + 1)
                    v.max(top[:, :], ndist[:, :]).then_inc(gap_ok, 1)
                    held(gap_ok, 5 * t + 2)
                    v.max_index(topi[:, :], top[:, :], ndist[:, :]).then_inc(gap_ok, 1)
                    v.tensor_tensor(gap[:, :], top[:, 1:2], top[:, 0:1], ALU.subtract).then_inc(gap_ok, 1)
                    wait(v, gap_ok, 5 * t + 4)
                    v.tensor_copy(topf[:, :], topi[:, 0:2]).then_inc(gap_ok, 1)
                    wait(v, gap_ok, 5 * t + 5)
                    wait(v, second_ok, t + 1)
                    v.tensor_scalar(wsum[:, 0:1], second[:, :], 1.0, None, ALU.add).then_inc(gate_ok, 1)
                    v.tensor_scalar(gate1[:, :], iota[:, :], topf[:, 1:2], second[:, 0:1], ALU.is_equal, ALU.mult)\
                        .then_inc(gate_ok, 1)
                    wait(v, gate_ok, 4 * t + 2)
                    v.reciprocal(wsum[:, 1:2], wsum[:, 0:1]).then_inc(gate_ok, 1)
                    wait(v, hgT_ps, t)
                    v.scalar_tensor_tensor(out=hg[:, R2:], in0=iota[:, :], scalar=topf[:, 0:1], in1=gate1[:, :],
                                           op0=ALU.is_equal, op1=ALU.add).then_inc(gate_ok, 1)
                    wait(v, gate_ok, 4 * t + 4)
                    wait(v, fh_ps, t + 1)
                    v.tensor_tensor(hg[:, 0:R2].rearrange("p (e r) -> p e r", r=RANK),
                                    PS[:, 7, :].rearrange("p (e r) -> p e r", r=RANK),
                                    bc(hg[:, R2:].unsqueeze(2), [P, PROTO, RANK]), ALU.mult).then_inc(hg_ok, 1)
                if s.has("P"):
                    t = s.tile("P")
                    wait(v, ke_ok, t + 1)
                    v.tensor_scalar(kp[:, :], ke[:, :], FEATURE_EPS, None, ALU.add).then_inc(kp_ok, 1)
                    wait(v, tdq_ps, t + 1)
                    v.tensor_reduce(qmx[:, :].rearrange("p (b h) -> p b h", b=2), td(4), AX_X, ALU.max)\
                        .then_inc(qb_ok, 1)
                    wait(v, qb_ok, 2 * t + 1)
                    v.tensor_tensor(qb[:, :], qmx[:, :], kb[:, H:], ALU.add).then_inc(qb_ok, 1)
                    wait(v, qb_ok, 2 * t + 2)
                    wait(v, qe_ok, t)
                    v.tensor_tensor(heads(qd), td(4), per_head(qb[:, :]), ALU.subtract).then_inc(qd_ok, 1)
                if s.has("M"):
                    t = s.tile("M")
                    wait(v, y2_ps, t + 1)
                    wait(v, hb_ok, t + 1)
                    wait(v, stored, 16 * t)
                    v.tensor_tensor(outb[:, :], PS[:, 1, 0:D], hb[:, :], ALU.add).then_inc(out_ok, 1)
                if s.has("P"):
                    t = s.tile("P")
                    wait(v, ctx_ps, t + 1)
                    v.tensor_tensor(ctxt[:, :, :], PS[0:MP, 6, 0:H * VA].rearrange("p (a b) -> p a b", a=HP),
                                    pair_mask[:, :, :], ALU.mult).then_inc(ctx_ok, 1)
                if s.has("E"):
                    t = s.tile("E")
                    norm_stats("E", t, esum[:, :], e_sum, 2 * t + 2)
                    norm_apply("E", t, esum[:, :], ehat[:, :])
                    norm_stats("P", t, h_of(t), e_out, 2 * t + 2)
                    wait(v, xT_ps["P"], s.after("P"))
                    norm_apply("P", t, h_of(t), xn["P"][:, :])
                if s.has("F"):
                    t = s.tile("F")
                    wait(v, y_ps, t + 1)
                    v.scalar_tensor_tensor(out=h_of(t), in0=PS[:, 7, 0:D], scalar=wsum[:, 1:2], in1=h_of(t),
                                           op0=ALU.mult, op1=ALU.add).then_inc(hF_ok, 1)
                    norm_stats("R", t, h_of(t), hF_ok, t + 1)
                    wait(v, xT_ps["R"], s.after("R"))
                    norm_apply("R", t, h_of(t), xn["R"][:, :])
                if s.has("P"):
                    t = s.tile("P")
                    wait(v, o_ps, t + 1)
                    o = PS[:, 4, 0:H * VA].rearrange("p (h d) -> p h d", d=VA)
                    v.reciprocal(oden[:, :], o[:, :, DH]).then_inc(o_ok, 1)
                    wait(v, o_ok, 2 * t + 1)
                    wait(v, oT_ps, t)
                    v.tensor_tensor(onorm[:, :].rearrange("p (h d) -> p h d", d=DH), o[:, :, 0:DH],
                                    bc(oden[:, :].unsqueeze(2), [P, H, DH]), ALU.mult).then_inc(o_ok, 1)
                if s.has("R"):
                    t = s.tile("R")
                    wait(v, pv_ps, t + 1)
                    o = PS[:, 5, 0:H * VA].rearrange("p (h d) -> p h d", d=VA)
                    v.reciprocal(rden[:, :], o[:, :, DH]).then_inc(ro_ok, 1)
                    wait(v, ro_ok, 2 * t + 1)
                    wait(v, roT_ps, t)
                    v.tensor_tensor(rout[:, :].rearrange("p (h d) -> p h d", d=DH), o[:, :, 0:DH],
                                    bc(rden[:, :].unsqueeze(2), [P, H, DH]), ALU.mult).then_inc(ro_ok, 1)
                if s.has("P"):
                    t = s.tile("P")
                    wait(v, of_ps, t + 1)
                    v.tensor_tensor(ofb[:, :], PS[:, 5, 0:D], bof[:, :], ALU.add).then_inc(hP_ok, 1)
                    wait(v, hP_ok, 2 * t + 1)
                    v.scalar_tensor_tensor(out=h_of(t), in0=ofb[:, :], scalar=0.0, in1=h_of(t),
                                           op0=ALU.max, op1=ALU.add).then_inc(hP_ok, 1)
                    norm_stats("F", t, h_of(t), hP_ok, 2 * t + 2)
                    wait(v, xT_ps["F"], s.after("F"))
                    wait(v, x2_ok, s.after("F"))
                    norm_apply("F", t, h_of(t), xn["F"][:, :])
                if s.has("R"):
                    t = s.tile("R")
                    wait(v, wo_ps, t + 1)
                    v.tensor_tensor(h_of(t), PS[:, 7, 0:D], h_of(t), ALU.add).then_inc(hR_ok, 1)
                    norm_stats("M", t, h_of(t), hR_ok, t + 1)
                    wait(v, xT_ps["M"], s.after("M"))
                    norm_apply("M", t, h_of(t), xn["M"][:, :])

            step(Step(-1))
            setup_p()
            step(Step(0))
            setup_f()
            step(Step(1))
            setup_rm()
            for i in range(2, LOOP_FROM):
                step(Step(i))
            with v.Fori(LOOP_FROM, LOOP_TO) as i:
                step(Step(i))
            for i in range(LOOP_TO, LAST_STEP + 1):
                step(Step(i))

        @block.scalar
        def _(a):
            def copy(dst, src, bias=0.0):
                return a.activation(dst, src, ACT.Identity if bias else ACT.Copy, bias=bias)

            def step(s):
                for x, bank in (("P", 7), ("R", 5)):
                    if s.has(x):
                        t = s.tile(x)
                        wait(a, xT_ps[x], t + 1)
                        wait(a, v_ps if x == "P" else rv_ps, t)
                        copy(xT[x][:, :, :], PS[:, bank, 0:D].rearrange("p (c n) -> p c n", c=KC))\
                            .then_inc(xT_ok[x], 1)
                if s.has("M"):
                    t = s.tile("M")
                    wait(a, xT_ps["M"], t + 1)
                    wait(a, m_ps, t)
                    copy(xhi[:, :, :], PS[:, 5, 0:D].rearrange("p (c n) -> p c n", c=KC)).then_inc(xT_ok["M"], 1)
                if s.has("R"):
                    t = s.tile("R")
                    wait(a, rv_ps, t + 1)
                    wait(a, pv_ps, t)
                    if s.static:
                        a.wait_ge(tern_abs, 2)
                    copy(rva[:, :, 0:DH], PS[:, 0, 0:D].rearrange("p (h d) -> p h d", d=DH)).then_inc(rv_ok, 1)
                if s.has("F"):
                    t = s.tile("F")
                    wait(a, xT_ps["F"], t + 1)
                    wait(a, fh_ps, t)
                    copy(xT["F"][:, :, :], PS[:, 1, 0:D].rearrange("p (c n) -> p c n", c=KC)).then_inc(xT_ok["F"], 1)
                    wait(a, ln_v["F"], 3 * t + 3)
                    wait(a, d2_ok, t)
                    a.activation(xsq[:, :], xn["F"][:, :], ACT.Square, accum_out=x2[:, 0:1]).then_inc(x2_ok, 1)
                if s.has("P"):
                    t = s.tile("P")
                    wait(a, qk_ok, t + 1)
                    wait(a, kb_ps, t)
                    a.activation(sqT[:, :, :], qkT[:, :, :], ACT.Square).then_inc(sq_ok, 1)
                if s.has("M"):
                    t = s.tile("M")
                    wait(a, m_ps, t + 1)
                    wait(a, y2_ps, t)
                    for m in range(FC):
                        last = a.activation(mh[:, m, :], PS[:, 2 + m // 4, m % 4 * P:(m % 4 + 1) * P], ACT.Relu,
                                            bias=b1[:, m:m + 1])
                    last.then_inc(mh_ok, 1)
                if s.has("R"):
                    t = s.tile("R")
                    wait(a, rT_ps, t + 1)
                    wait(a, s2_ps, t)
                    copy(rT[:, :, :], PS[:, 0:2, :].rearrange("p b (c n) -> p (b c) n", c=4)).then_inc(rT_ok, 1)
                if s.has("P"):
                    t = s.tile("P")
                    wait(a, kb_ps, t + 1)
                    wait(a, qb_ok, 2 * t)
                    wait(a, kd_ok, t)
                    copy(kb[:, :], PS[:, 6, 0:2 * H]).then_inc(kb_ok, 1)
                if s.has("F"):
                    t = s.tile("F")
                    wait(a, gap_ok, 5 * t + 4)
                    wait(a, gate_ok, 4 * t)
                    a.activation(second[:, :], gap[:, :], ACT.Exp).then_inc(second_ok, 1)
                if s.has("P"):
                    t = s.tile("P")
                    wait(a, kd_ok, t + 1)
                    wait(a, kp_ok, t)
                    a.activation(ke[:, :], kd[:, :], ACT.Exp).then_inc(ke_ok, 1)
                if s.has("R"):
                    t = s.tile("R")
                    wait(a, rqT_ps, t + 1)
                    wait(a, s2_ps, t)
                    copy(rqT[:, :, :], PS[:, 0, :].rearrange("p (c n) -> p c n", c=4)).then_inc(rqT_ok, 1)
                if s.has("P"):
                    t = s.tile("P")
                    wait(a, qd_ok, t + 1)
                    wait(a, qp_ps, t)
                    a.activation(qe[:, :], qd[:, :], ACT.Exp).then_inc(qe_ok, 1)
                if s.has("F"):
                    t = s.tile("F")
                    wait(a, hgT_ps, t + 1)
                    wait(a, y_ps, t)
                    copy(hgT[:, :, :], PS[:, 7, :].rearrange("p (c n) -> p c n", c=4)).then_inc(hgT_ok, 1)
                    copy(gT[:, :], PS[0:PROTO, 6, 0:P]).then_inc(hgT_ok, 1)
                if s.has("R"):
                    t = s.tile("R")
                    wait(a, s2_ps, t + 1)
                    wait(a, pv_ps, t)
                    for b in (0, 2):
                        a.activation(pT[:, b:b + 2, :, :], PS[:, b:b + 2, :].rearrange("p j (c q) -> p j c q", c=4),
                                     ACT.Exp).then_inc(pT_ok, 1)
                if s.has("P"):
                    t = s.tile("P")
                    wait(a, qp_ps, t + 1)
                    wait(a, o_ps, t)
                    copy(qp[:, :, :], PS[0:MP, 4:6, :].rearrange("p b (c n) -> p (b c) n", c=4), FEATURE_EPS)\
                        .then_inc(qp_ok, 1)
                    wait(a, oT_ps, t + 1)
                    wait(a, of_ps, t)
                    copy(oT[:, :, :], PS[:, 7, 0:D].rearrange("p (c n) -> p c n", c=KC)).then_inc(oT_ok, 1)
                if s.has("R"):
                    t = s.tile("R")
                    wait(a, roT_ps, t + 1)
                    wait(a, wo_ps, t)
                    copy(roT[:, :, :], PS[:, 4, 0:D].rearrange("p (c n) -> p c n", c=KC)).then_inc(roT_ok, 1)

            a.wait_ge(load["M"], 16 * N_LOAD["M"])
            for i in range(FIRST_STEP, LOOP_FROM):
                step(Step(i))
            with a.Fori(LOOP_FROM, LOOP_TO) as i:
                step(Step(i))
            for i in range(LOOP_TO, LAST_STEP + 1):
                step(Step(i))

        @block.tensor
        def _(pe):
            def transpose2(bank, x):
                for c in range(KC):
                    last = pe.transpose(PS[:, bank, c * P:(c + 1) * P], x[:, c * P:(c + 1) * P], ident[:, :])
                return last

            def token_major(dst, x, w):
                for c in range(KC):
                    last = pe.matmul(dst, x[:, c, :], w[:, c, :], start=(c == 0), stop=(c == KC - 1))
                return last

            def features(bank, c0):
                for c in range(KC):
                    last = pe.matmul(PS[:, bank + c, 0:8 * M], qkT[:, c0 + c, :], proj[:, :], start=True, stop=True)
                return last

            def step(s):
                P_, F_, R_, M_ = (s.has(x) for x in "PFRM")
                p, f, r, m = (s.tile(x) for x in "PFRM")
                if P_:
                    wait(pe, ln_v["P"], 3 * p + 3)
                    wait(pe, hR_ok, s.before("R"))
                    transpose2(7, xn["P"]).then_inc(xT_ps["P"], 1)
                if R_:
                    wait(pe, ln_v["R"], 3 * r + 3)
                    wait(pe, hP_ok, 2 * s.before("P"))
                    transpose2(5, xn["R"]).then_inc(xT_ps["R"], 1)
                    wait(pe, xT_ok["R"], r + 1)
                    wait(pe, roT_ok, r)
                    wait(pe, o_ok, 2 * s.before("P"))
                    token_major(PS[:, 4, :], xT["R"], rwqk).then_inc(rqk_ps, 1)
                if P_:
                    wait(pe, xT_ok["P"], p + 1)
                    for j in range(4):
                        for c in range(KC):
                            last = pe.matmul(PS[:, 7, j * P:(j + 1) * P], wqkT[:, c, j * P:(j + 1) * P],
                                             xT["P"][:, c, :], start=(c == 0), stop=(c == KC - 1))
                    last.then_inc(qk_ps, 1)
                if M_:
                    wait(pe, ln_v["M"], 3 * m + 3)
                    wait(pe, xT_ok["R"], s.after("R"))
                    wait(pe, hP_ok, 2 * s.before("P"))
                    transpose2(5, xn["M"]).then_inc(xT_ps["M"], 1)
                if R_:
                    wait(pe, pT_ok, 2 * r)
                    token_major(PS[:, 0, 0:D], xT["R"], rwv).then_inc(rv_ps, 1)
                if F_:
                    wait(pe, ln_v["F"], 3 * f + 3)
                    wait(pe, pT_ok, 2 * s.before("R"))
                    transpose2(1, xn["F"]).then_inc(xT_ps["F"], 1)
                if M_:
                    if s.static:
                        pe.wait_ge(tern, 9)
                    wait(pe, xT_ok["M"], m + 1)
                    wait(pe, xlo_ok, m + 1)
                    wait(pe, pT_ok, 2 * s.before("R"))
                    for j in range(FC):
                        n = 0
                        for part in (xhi, xlo):
                            for c in range(KC):
                                last = pe.matmul(PS[:, 2 + j // 4, j % 4 * P:(j % 4 + 1) * P],
                                                 w1q[:, c, j * P:(j + 1) * P], part[:, c, :],
                                                 start=(n == 0), stop=(n == 3))
                                n += 1
                    last.then_inc(m_ps, 1)
                if R_:
                    wait(pe, rot_ok, r + 1)
                    wait(pe, rv_ok, r + 1)
                    wait(pe, xT_ok["F"], s.after("F"))
                    for c in range(8):
                        last = pe.transpose(PS[:, c // 4, c % 4 * P:(c % 4 + 1) * P],
                                            rpad[:, 4 * c:4 * c + 4, :].rearrange("p h d -> p (h d)"), ident[:, :])
                    last.then_inc(rT_ps, 1)
                if P_:
                    wait(pe, qk_ok, p + 1)
                    token_major(PS[:, 7, 0:D], xT["P"], wvT).then_inc(v_ps, 1)
                    wait(pe, rope_ok, 3 * s.after("R"))
                    wait(pe, xlo_ok, s.after("M"))
                    wait(pe, xT_ok["M"], s.after("M"))
                    features(4, 2).then_inc(tdk_ps, 1)
                if F_:
                    wait(pe, xT_ok["F"], f + 1)
                    wait(pe, v_ok, s.after("P"))
                    wait(pe, hF_ok, f)
                    token_major(PS[:, 7, :], xT["F"], fbT).then_inc(fh_ps, 1)
                if P_:
                    wait(pe, kmx_ok, p + 1)
                    wait(pe, ctx_ok, s.before("P"))
                    wait(pe, hgT_ok, 2 * s.before("F"))
                    pe.transpose(PS[0:H, 6, 0:P], kmx[:, :], ident[:, :]).then_inc(kmxT_ps, 1)
                if R_:
                    wait(pe, rT_ok, r + 1)
                    wait(pe, mh_ok, s.after("M"))
                    for j in range(4):
                        pe.matmul(PS[:, j, :], ident_b[:, :], mask_qk[:, :, :].rearrange("p c k -> p (c k)"),
                                  start=True, stop=False, skip_group_check=True)
                if F_:
                    wait(pe, kdiag_ok, 2 * s.after("P"))
                    wait(pe, hgT_ok, 2 * f)
                    for c in range(KC):
                        pe.matmul(PS[:, 6, 0:PROTO], xT["F"][:, c, :], protoT2[:, c, :], start=(c == 0), stop=False)
                    pe.matmul(PS[:, 6, 0:PROTO], ones[0:1, :], p2[0:1, :], start=False, stop=True)\
                        .then_inc(proto_ps, 1)
                if R_:
                    for c in range(4):
                        for j in range(4):
                            o = SLOT * j
                            last = pe.matmul(PS[:, j, c * P:(c + 1) * P], rT[o:o + DH, c, :], rT[o:o + DH, 4 + c, :],
                                             start=False, stop=True, skip_group_check=True)
                    last.then_inc(s1_ps, 1)
                if P_:
                    wait(pe, sq_ok, p + 1)
                    wait(pe, kdiag_ok, 2 * p + 2)
                    wait(pe, d2_ok, s.after("F"))
                    for c in range(KC):
                        pe.matmul(PS[:, 6, 0:H], sqT[:, 2 + c, :], half_sq[:, c, :], start=(c == 0), stop=False)
                    pe.matmul(PS[:, 6, 0:H], ones[0:H, :], kdiag[:, :], start=False, stop=True)
                    for c in range(KC):
                        last = pe.matmul(PS[:, 6, H:2 * H], sqT[:, c, :], half_sq[:, c, :],
                                         start=(c == 0), stop=(c == KC - 1))
                    last.then_inc(kb_ps, 1)
                    wait(pe, kd_ok, p + 1)
                    features(4, 0).then_inc(tdq_ps, 1)
                if R_:
                    wait(pe, rmax_ok, r + 1)
                    for c in range(4):
                        last = pe.transpose(PS[:, 0, c * P:(c + 1) * P],
                                            rpad[:, 4 * c:4 * c + 4, :].rearrange("p h d -> p (h d)"), ident[:, :])
                    last.then_inc(rqT_ps, 1)
                if M_:
                    wait(pe, mh_ok, m + 1)
                    wait(pe, rmax_ok, s.after("R"))
                    wait(pe, xT_ok["F"], s.after("F"))
                    for j in range(FC):
                        last = pe.matmul(PS[:, 1, 0:D], mh[:, j, :], w2q[:, j, :], start=(j == 0), stop=(j == FC - 1))
                    last.then_inc(y2_ps, 1)
                if F_:
                    wait(pe, hg_ok, f + 1)
                    wait(pe, kb_ok, s.after("P"))
                    for c in range(R2 // P):
                        pe.transpose(PS[:, 7, c * P:(c + 1) * P], hg[:, c * P:(c + 1) * P], ident[:, :])
                    pe.transpose(PS[0:PROTO, 6, 0:P], hg[:, R2:], ident[:, :]).then_inc(hgT_ps, 1)
                if R_:
                    wait(pe, rqT_ok, r + 1)
                    wait(pe, out_ok, s.after("M"))
                    for j in range(4):
                        pe.matmul(PS[:, j, :], ident_b[:, :], mask_kq[:, :, :].rearrange("p c k -> p (c k)"),
                                  start=True, stop=False, skip_group_check=True)
                    for c in range(4):
                        for j in range(4):
                            o = SLOT * j
                            last = pe.matmul(PS[:, j, c * P:(c + 1) * P], rT[o:o + VA, 4 + c, :], rqT[o:o + VA, c, :],
                                             start=False, stop=True, skip_group_check=True)
                    last.then_inc(s2_ps, 1)
                if P_:
                    wait(pe, qe_ok, p + 1)
                    for j in range(HP):
                        last = pe.transpose(PS[0:MP, 4 + j // 4, j % 4 * P:(j % 4 + 1) * P],
                                            qe[:, j * MP:(j + 1) * MP], ident[:, :])
                    last.then_inc(qp_ps, 1)
                    wait(pe, kp_ok, p + 1)
                    wait(pe, v_ok, p + 1)
                    wait(pe, hgT_ok, 2 * s.after("F"))
                    wait(pe, kb_ok, p + 1)
                    for j in range(HP):
                        last = pe.matmul(PS[0:MP, 6, 2 * VA * j:2 * VA * (j + 1)],
                                         kp[:, j * MP:(j + 1) * MP],
                                         va[:, 2 * j:2 * j + 2, :].rearrange("p h d -> p (h d)"), start=True, stop=True)
                    last.then_inc(ctx_ps, 1)
                if F_:
                    wait(pe, hgT_ok, 2 * f + 2)
                    for c in range(R2 // P):
                        pe.matmul(PS[:, 7, 0:D], hgT[:, c, :], faT[:, c, :], start=(c == 0), stop=False)
                    pe.matmul(PS[:, 7, 0:D], gT[:, :], fbias[:, :], start=False, stop=True).then_inc(y_ps, 1)
                if P_:
                    wait(pe, qp_ok, p + 1)
                    wait(pe, ctx_ok, p + 1)
                    for j in range(HP):
                        last = pe.matmul(PS[:, 4, 2 * VA * j:2 * VA * (j + 1)], qp[:, j, :], ctxt[:, j, :],
                                         start=True, stop=True)
                    last.then_inc(o_ps, 1)
                if R_:
                    wait(pe, qp_ok, s.after("P"))
                    for j in range(4):
                        wait(pe, pT_ok, 2 * r + 1 + j // 2)
                        for c in range(4):
                            h = 4 * c + j
                            last = pe.matmul(PS[:, 5, VA * h:VA * (h + 1)], pT[:, j, c, :], rva[:, h, :],
                                             start=True, stop=True)
                    last.then_inc(pv_ps, 1)
                if P_:
                    wait(pe, o_ok, 2 * p + 2)
                    wait(pe, hF_ok, s.after("F"))
                    transpose2(7, onorm).then_inc(oT_ps, 1)
                if R_:
                    wait(pe, ro_ok, 2 * r + 2)
                    wait(pe, o_ok, 2 * s.after("P"))
                    transpose2(4, rout).then_inc(roT_ps, 1)
                if P_:
                    wait(pe, oT_ok, p + 1)
                    wait(pe, ro_ok, 2 * s.after("R"))
                    token_major(PS[:, 5, 0:D], oT, wof).then_inc(of_ps, 1)
                if R_:
                    wait(pe, roT_ok, r + 1)
                    wait(pe, oT_ok, s.after("P"))
                    wait(pe, hF_ok, s.after("F"))
                    token_major(PS[:, 7, 0:D], roT, rwo).then_inc(wo_ps, 1)

            pe.wait_ge(g_const, 17)
            pe.wait_ge(load["P"], 16 * N_LOAD["P"])
            for i in range(KC):
                for c in range(KC):
                    last = pe.matmul(PS[:, 4 + i, 0:D], wo[:, c, i * P:(i + 1) * P], wfcT[:, c, :],
                                     start=(c == 0), stop=(c == KC - 1))
                last.then_inc(wof_ps, 1)
            for c in range(KC):
                last = pe.matmul(PS[:, 6, 0:D], bo[:, c:c + 1].to_broadcast([P, P]), wfcT[:, c, :],
                                 start=(c == 0), stop=(c == KC - 1))
            last.then_inc(wof_ps, 1)
            pe.wait_ge(wof_ok, 2)
            pe.wait_ge(s_const, 2)
            step(Step(0))
            pe.wait_ge(p2_ok, 2)
            pe.wait_ge(ctx_ok, 1)
            for c in range(KC):
                last = pe.matmul(PS[0:1, 6, 0:PROTO], ones[:, 0:1], proto_sq[:, c, :],
                                 start=(c == 0), stop=(c == KC - 1))
            last.then_inc(p2_ps, 1)
            pe.wait_ge(p2_ok, 8)
            step(Step(1))
            pe.wait_ge(tern_abs, 10)
            pe.wait_ge(ctx_ok, 2)
            pe.wait_ge(hgT_ok, 2)
            pe.matmul(PS[:, 6, 0:2], ones[:, :], absum[:, :], start=True, stop=True).then_inc(tern_ps, 1)
            pe.wait_ge(tern, 1)
            for i in range(2, LOOP_FROM):
                step(Step(i))
            with pe.Fori(LOOP_FROM, LOOP_TO) as i:
                step(Step(i))
            for i in range(LOOP_TO, LAST_STEP + 1):
                step(Step(i))


def rotary_tables():
    inv = (np.float32(1.0) / np.power(np.float32(10000.0), np.arange(0, DH, 2, dtype=np.float32) / np.float32(DH)))
    theta = np.arange(P, dtype=np.float32)[:, None] * inv.astype(np.float32)[None, :]
    cos, sin = np.cos(theta).astype(np.float32), np.sin(theta).astype(np.float32)
    signed = np.stack([-sin, sin], axis=-1).reshape(P, DH)
    return np.tile(np.repeat(cos, 2, axis=-1), (1, 2 * H)), np.tile(signed, (1, 2 * H))


def kernel(**inputs):
    import concourse.bacc as _bacc
    from concourse.bass_utils import run_bass_kernel_spmd as _run

    a = {k: np.asarray(x) for k, x in inputs.items()}

    def cols(x, n):
        return x.reshape(n, P).T

    cos, sin = rotary_tables()
    laid = {
        "ids": np.stack([a["x"].T, a["itok_BS_0_511"].T, a["mask_BS_i1_0"].T], axis=1),
        "word": a["L0_tok_word_emb"], "pos": a["L0_tok_pos_emb"], "type": a["L0_tok_type_emb"],
        "gamma": a["L0_tok_ln_gamma"], "beta": a["L0_tok_ln_beta"],
        "wqkT": np.concatenate([a["L0_attn_Wq"].T, a["L0_attn_Wk"].T], axis=1), "wvT": a["L0_attn_Wv"].T,
        "wo": a["L0_attn_Wo"], "wfcT": a["L0_attn_Wfc"].T,
        "bqk": cols(np.concatenate([a["L0_attn_bq"], a["L0_attn_bk"]]), 4), "bv": a["L0_attn_bv"],
        "bo": cols(a["L0_attn_bo"], KC), "bfc": a["L0_attn_bfc"], "projT": a["L0_attn_proj"].T,
        "protoT": a["L0_ffn_prototypes"].T, "fbT": a["L0_ffn_B"].reshape(R2, D).T,
        "faT": a["L0_ffn_A"].transpose(0, 2, 1).reshape(R2, D), "fbias": a["L0_ffn_bias"],
        "temp": a["L0_ffn_temp"].reshape(1),
        "rwqk": np.concatenate([a["L1_attn_Wq"], a["L1_attn_Wk"]], axis=1), "rwv": a["L1_attn_Wv"],
        "rwo": a["L1_attn_Wo"], "rope_cos": cos, "rope_sin": sin,
        "w1T": a["L1_ffn_W1"].T, "w2T": a["L1_ffn_W2"].T, "b1": cols(a["L1_ffn_b1"], FC), "b2": a["L1_ffn_b2"],
    }
    nc = _bacc.Bacc("TRN2", target_bir_lowering=False, num_devices=1)
    arrays, aps = {}, {}
    for name, x in laid.items():
        x = np.ascontiguousarray(x)
        arrays[f"in_{name}"] = x
        aps[name] = nc.dram_tensor(f"in_{name}", x.shape, mybir.dt.from_np(x.dtype), kind="ExternalInput").ap()
    out = nc.dram_tensor("out_0", (TILES, P, D), F32, kind="ExternalOutput").ap()
    program(nc, aps, out)
    r = _run(nc, [arrays], core_ids=[0])
    return r.results[0]["out_0"]
```

```python
from contextlib import ExitStack

import numpy as np

import concourse.bass as bass
from concourse import mybir

ALU = mybir.AluOpType
ACT = mybir.ActivationFunctionType
F32 = mybir.dt.float32
F16 = mybir.dt.float16
BF16 = mybir.dt.bfloat16
I32 = mybir.dt.int32
U32 = mybir.dt.uint32
AX_X = mybir.AxisListType.X

P = 128
D = 256
KC = D // P
TILES = 16
H = 16
DH = D // H
M = 44
HP = H // 2
MP = 2 * M
VA = DH + 1
PROTO = 32
RANK = 16
R2 = PROTO * RANK
F1 = 1024
FC = F1 // P
VOCAB, POS, TYPES = 30522, 128, 2
FEATURE_EPS = 1e-4
EMB_EPS, LN_EPS, QUANT_EPS = 1e-12, 1e-5, 1e-5
HIDDEN_SCORE = -1e30
SLOT = 64
PARTS = 3 * DH
KEYS = H * SLOT + DH
SPLIT_W = KEYS + H * SLOT
WS = 256.0

SKEW = {"E": -1, "P": 0, "F": 1, "R": 2, "M": 3}
FIRST_STEP, LAST_STEP = -1, TILES - 1 + SKEW["M"]
LOOP_FROM, LOOP_TO = SKEW["M"] + 1, TILES - 2


class Step:

    def __init__(self, i):
        self.i = i
        self.static = isinstance(i, int)
        self.first = self.static and i == FIRST_STEP

    def has(self, stage):
        return not self.static or 0 <= self.i - SKEW[stage] < TILES

    def tile(self, stage):
        return self.i - SKEW[stage]

    def before(self, stage):
        t = self.i - SKEW[stage]
        return min(max(t, 0), TILES) if self.static else t

    def after(self, stage):
        return self.before(stage) + (1 if self.has(stage) else 0)

    def next_gather(self):
        return not self.static or 0 <= self.i + 2 < TILES


def wait(eng, sem, count):
    if not (isinstance(count, int) and count <= 0):
        eng.wait_ge(sem, count)


def program(nc, A, out):
    with ExitStack() as ctx:
        def sb(name, shape, dt=F32):
            return ctx.enter_context(nc.sbuf_tensor(name, shape, dt))

        def sem(name):
            return ctx.enter_context(nc.semaphore(name))

        PS = ctx.enter_context(nc.psum_tensor("PS", [P, 8, 512], F32))

        ids = sb("ids", [P, 3, TILES], I32)
        ids_neg = sb("ids_neg", [P, 3, TILES], I32)
        idx = sb("idx", [P, 3], I32)
        gamma = sb("gamma", [P, D])
        beta = sb("beta", [P, D])
        wqkT = sb("wqkT", [P, KC, 2 * D])
        wvT = sb("wvT", [P, KC, D])
        wo = sb("wo", [P, KC, D])
        wfcT = sb("wfcT", [P, KC, D])
        wof = sb("wof", [P, KC, D])
        bqk = sb("bqk", [P, 4])
        bv = sb("bv", [P, D])
        bo = sb("bo", [P, KC])
        bfc = sb("bfc", [P, D])
        bof = sb("bof", [P, D])
        proj = sb("proj", [P, 8 * M])
        half_sq = sb("half_sq", [P, KC, H])
        ones = sb("ones", [P, P])
        ident = sb("ident", [P, P])
        ident_b = sb("ident_b", [P, P], BF16)
        ident_h = sb("ident_h", [P, P], F16)
        head_row = sb("head_row", [H, H, P], F16)
        pair_mask = sb("pair_mask", [MP, HP, 2 * VA])
        protoT = sb("protoT", [P, KC, PROTO])
        protoT2 = sb("protoT2", [P, KC, PROTO])
        proto_sq = sb("proto_sq", [P, KC, PROTO])
        p2 = sb("p2", [1, PROTO])
        fbT = sb("fbT", [P, KC, R2])
        faT = sb("faT", [P, R2 // P, D])
        fbias = sb("fbias", [PROTO, D])
        temp = sb("temp", [P, 4])
        iota_i = sb("iota_i", [P, PROTO], I32)
        iota = sb("iota", [P, PROTO])
        consts = sb("consts", [P, 4])
        halves = sb("halves", [P, 2])
        rope_cos = sb("rope_cos", [P, 2 * D])
        rope_sin = sb("rope_sin", [P, 2 * D])
        rwqk = sb("rwqk", [P, KC, 2 * D])
        rwv = sb("rwv", [P, KC, D])
        rwo = sb("rwo", [P, KC, D])
        mask_f = sb("mask_f", [P, 2, P])
        mask_qk = sb("mask_qk", [P, 4, P], BF16)
        mask_kq = sb("mask_kq", [P, 4, P], BF16)
        SPLITS = {"wqkT": (wqkT, 2 * D), "wvT": (wvT, D), "fbT": (fbT, R2), "protoT2": (protoT2, PROTO),
                  "rwqk": (rwqk, 2 * D), "rwv": (rwv, D)}
        whi = {k: sb(f"{k}_hi", [P, KC, n], F16) for k, (_, n) in SPLITS.items()}
        wlo = {k: sb(f"{k}_lo", [P, KC, n], F16) for k, (_, n) in SPLITS.items()}
        w1 = sb("w1", [P, KC * F1])
        w2 = sb("w2", [P, FC * D])
        wneg = sb("wneg", [P, F1])
        w1q = sb("w1q", [P, KC, F1], F16)
        w2q = sb("w2q", [P, FC, D], F16)
        absum = sb("absum", [P, 2])
        thr = sb("thr", [P, 4])
        b1 = sb("b1", [P, FC])
        b2 = sb("b2", [P, D])

        hres = sb("hres", [P, TILES, D])

        def slots(o):
            return split[:, 0:2 * H * SLOT].rearrange("p (h s) -> p h s", s=SLOT)[:, :, o:o + DH]

        def h_of(t):
            return hres[:, bass.ds(t, 1), :].rearrange("p a n -> p (a n)")

        emb = sb("emb", [P, 3, D])
        esum1 = sb("esum1", [P, D])
        esum = sb("esum", [P, D])
        ehat = sb("ehat", [P, D])
        escaled = sb("escaled", [P, D])

        LNS = ("E", "P", "F", "R", "M")
        stats = {x: sb(f"stats{x}", [P, 6]) for x in LNS}
        mv = {x: sb(f"mv{x}", [P, 2]) for x in LNS}
        rstd = {x: sb(f"rstd{x}", [P, 2]) for x in LNS}
        xn = {x: sb(f"xn{x}", [P, D]) for x in "PFRM"}
        xhi = {x: sb(f"xhi{x}", [P, KC, P], F16) for x in "PFRM"}
        xlo = {x: sb(f"xlo{x}", [P, KC, P], F16) for x in "PFRM"}

        qkT = sb("qkT", [P, 4, P])
        sqT = sb("sqT", [P, 4, P])
        va = sb("va", [P, H, VA])
        kmx = sb("kmx", [P, H])
        kmx_row = sb("kmx_row", [H, 1])
        kdiag = sb("kdiag", [H, H])
        kb = sb("kb", [P, 2 * H])
        kd = sb("kd", [P, H * M])
        ke = sb("ke", [P, H * M])
        kp = sb("kp", [P, H * M])
        ctxt = sb("ctxt", [MP, HP, 2 * VA])
        qmx = sb("qmx", [P, H])
        qb = sb("qb", [P, H])
        qd = sb("qd", [P, H * M])
        qe = sb("qe", [P, H * M])
        qp = sb("qp", [MP, HP, P])
        oden = sb("oden", [P, H])
        onorm = sb("onorm", [P, D])
        oT = sb("oT", [P, KC, P])
        ofb = sb("ofb", [P, D])

        xsq = sb("xsq", [P, D])
        x2 = sb("x2", [P, 1])
        nd2 = sb("nd2", [P, PROTO])
        near = sb("near", [P, 2])
        dist = sb("dist", [P, 2])
        top = sb("top", [P, 8])
        topi = sb("topi", [P, 8], U32)
        topf = sb("topf", [P, 2])
        gap = sb("gap", [P, 1])
        second = sb("second", [P, 1])
        wsum = sb("wsum", [P, 2])
        gate1 = sb("gate1", [P, PROTO])
        hg = sb("hg", [P, R2 + PROTO])
        hgT = sb("hgT", [P, R2 // P, P])
        gT = sb("gT", [PROTO, P])

        rc = sb("rc", [P, 2 * D])
        rs = sb("rs", [P, 2 * D])
        rot = sb("rot", [P, 2 * H, DH])
        split = sb("split", [P, SPLIT_W], F16)
        vhi = sb("vhi", [P, H, VA], F16)
        vlo = sb("vlo", [P, H, VA], F16)
        rT = sb("rT", [P, 2 * H // 2, P], F16)
        negmax = sb("negmax", [P, H], F16)
        negmaxT = sb("negmaxT", [H, P], F16)
        phi = sb("phi", [P, 4, 4, P], F16)
        pfull = sb("pfull", [P, 4, 4, P])
        plo = sb("plo", [P, 4, 4, P], F16)
        rden = sb("rden", [P, H])
        rout = sb("rout", [P, D])
        roT = sb("roT", [P, KC, P])

        mh = sb("mh", [P, FC, P])
        mhi = sb("mhi", [P, FC, P], F16)
        mlo = sb("mlo", [P, FC, P], F16)
        hb = sb("hb", [P, D])
        outb = sb("outb", [P, D])

        ids_in = sem("ids_in"); load = {x: sem(f"weights_in_{x}") for x in "EPFRM"}
        proj_zero = sem("proj_zero"); proj_in = sem("proj_in")
        gathered = sem("gathered"); ids_ok = sem("ids_ok"); idx_ok = sem("idx_ok")
        g_const = sem("g_const"); v_const = sem("v_const"); s_const = sem("s_const")
        wof_ps = sem("wof_ps"); wof_ok = sem("wof_ok"); p2_ps = sem("p2_ps"); p2_ok = sem("p2_ok")
        tern_abs = sem("tern_abs"); tern_ps = sem("tern_ps"); tern = sem("tern")
        v_held = sem("v_held"); g_held = sem("g_held")
        ln_v = {x: sem(f"ln_v_{x}") for x in LNS}; ln_g = {x: sem(f"ln_g_{x}") for x in LNS}
        e_sum = sem("e_sum"); e_out = sem("e_out")
        xT_ps = {x: sem(f"xT_ps_{x}") for x in "PFRM"}; xT_ok = {x: sem(f"xT_ok_{x}") for x in "PFRM"}
        qk_ps = sem("qk_ps"); qk_ok = sem("qk_ok"); sq_ok = sem("sq_ok")
        v_ps = sem("v_ps"); v_ok = sem("v_ok")
        tdk_ps = sem("tdk_ps"); kmx_ok = sem("kmx_ok"); kmxT_ps = sem("kmxT_ps"); kdiag_ok = sem("kdiag_ok")
        kb_ps = sem("kb_ps"); kb_ok = sem("kb_ok"); kd_ok = sem("kd_ok"); ke_ok = sem("ke_ok"); kp_ok = sem("kp_ok")
        ctx_ps = sem("ctx_ps"); ctx_ok = sem("ctx_ok")
        tdq_ps = sem("tdq_ps"); qb_ok = sem("qb_ok"); qd_ok = sem("qd_ok"); qe_ok = sem("qe_ok")
        qp_ps = sem("qp_ps"); qp_ok = sem("qp_ok")
        o_ps = sem("o_ps"); o_ok = sem("o_ok"); oT_ps = sem("oT_ps"); oT_ok = sem("oT_ok")
        of_ps = sem("of_ps"); hP_ok = sem("hP_ok")
        x2_ok = sem("x2_ok"); fh_ps = sem("fh_ps"); proto_ps = sem("proto_ps"); d2_ok = sem("d2_ok")
        near_ok = sem("near_ok"); dist_ok = sem("dist_ok")
        gap_ok = sem("gap_ok"); second_ok = sem("second_ok"); gate_ok = sem("gate_ok"); hg_ok = sem("hg_ok")
        hgT_ps = sem("hgT_ps"); hgT_ok = sem("hgT_ok"); y_ps = sem("y_ps"); hF_ok = sem("hF_ok")
        rqk_ps = sem("rqk_ps"); rope_ok = sem("rope_ok"); rot_ok = sem("rot_ok")
        rv_ps = sem("rv_ps"); vhi_ok = sem("vhi_ok"); vlo_ok = sem("vlo_ok"); rT_ps = sem("rT_ps")
        rqT_ok = sem("rqT_ok"); rkT_ok = sem("rkT_ok"); rothi_ok = sem("rothi_ok"); rotlo_ok = sem("rotlo_ok")
        s1_ps = sem("s1_ps"); rmax_ok = sem("rmax_ok"); nmT_ps = sem("nmT_ps"); nmT_ok = sem("nmT_ok")
        s2_ps = sem("s2_ps"); phi_ok = sem("phi_ok"); plo_ok = sem("plo_ok"); pv_ps = sem("pv_ps"); ro_ok = sem("ro_ok")
        roT_ps = sem("roT_ps"); roT_ok = sem("roT_ok"); wo_ps = sem("wo_ps"); hR_ok = sem("hR_ok")
        xlo_ok = {x: sem(f"xlo_ok_{x}") for x in "PFRM"}; whi_ok = sem("whi_ok"); wlo_ok = sem("wlo_ok")
        m_ps = sem("m_ps"); mh_ok = sem("mh_ok"); mlo_ok = sem("mlo_ok"); hb_ok = sem("hb_ok")
        y2_ps = sem("y2_ps"); out_ok = sem("out_ok"); stored = sem("stored")

        N_LOAD = {"E": 2, "P": 8, "F": 5, "R": 5, "M": 4}
        G_CONST, V_CONST = 14, 9

        block = ctx.enter_context(nc.Block())

        @block.sync
        def _(sp):
            def get(x, dst, src):
                sp.dma_start(dst, src).then_inc(load[x], 16)

            sp.dma_start(ids[:, :, :], A["ids"]).then_inc(ids_in, 16)
            get("E", gamma[:, :], A["gamma"].partition_broadcast(P))
            get("E", beta[:, :], A["beta"].partition_broadcast(P))
            get("P", wqkT[:, :, :], A["wqkT"].rearrange("(c p) n -> p c n", p=P))
            get("P", wvT[:, :, :], A["wvT"].rearrange("(c p) n -> p c n", p=P))
            get("P", bqk[:, :], A["bqk"])
            get("P", bv[:, :], A["bv"].partition_broadcast(P))
            get("P", wo[:, :, :], A["wo"].rearrange("(c p) n -> p c n", p=P))
            get("P", wfcT[:, :, :], A["wfcT"].rearrange("(c p) n -> p c n", p=P))
            get("P", bo[:, :], A["bo"])
            get("P", bfc[:, :], A["bfc"].partition_broadcast(P))
            sp.wait_ge(proj_zero, 1)
            for j in range(8):
                sp.dma_start(proj[DH * j:DH * (j + 1), M * j:M * (j + 1)], A["projT"]).then_inc(proj_in, 16)
            get("F", protoT[:, :, :], A["protoT"].rearrange("(c p) n -> p c n", p=P))
            get("F", fbT[:, :, :], A["fbT"].rearrange("(c p) n -> p c n", p=P))
            get("F", faT[:, :, :], A["faT"].rearrange("(c p) n -> p c n", p=P))
            get("F", fbias[:, :], A["fbias"])
            get("F", temp[:, 0:1], A["temp"].partition_broadcast(P))
            get("R", rwqk[:, :, :], A["rwqk"].rearrange("(c p) n -> p c n", p=P))
            get("R", rwv[:, :, :], A["rwv"].rearrange("(c p) n -> p c n", p=P))
            get("R", rwo[:, :, :], A["rwo"].rearrange("(c p) n -> p c n", p=P))
            get("R", rope_cos[:, :], A["rope_cos"])
            get("R", rope_sin[:, :], A["rope_sin"])
            get("M", w1[:, :].rearrange("p (c n) -> p c n", c=KC), A["w1T"].rearrange("(c p) n -> p c n", p=P))
            get("M", w2[:, :].rearrange("p (c n) -> p c n", c=FC), A["w2T"].rearrange("(c p) n -> p c n", p=P))
            get("M", b1[:, :], A["b1"])
            get("M", b2[:, :], A["b2"].partition_broadcast(P))
            with sp.Fori(0, TILES) as t:
                sp.wait_ge(out_ok, t + 1)
                sp.dma_start(out[bass.ds(t, 1), :, :].rearrange("a p n -> p (a n)"), outb[:, :]).then_inc(stored, 16)
            sp.wait_ge(stored, 16 * TILES)

        @block.gpsimd
        def _(g):
            def held(sem_, count):
                wait(g, sem_, count)
                g.sem_inc(g_held, 1)

            tables = (A["word"], A["pos"], A["type"])

            def gather(t):
                held(idx_ok, t)
                g.tensor_copy(idx[:, :].unsqueeze(2), ids[:, :, bass.ds(t, 1)]).then_inc(idx_ok, 1)
                held(idx_ok, t + 1)
                for k in range(3):
                    g.indirect_dma_start(emb[:, k, :], None, tables[k],
                                         bass.IndirectOffsetOnAxis(idx[:, k:k + 1], 0)).then_inc(gathered, 16)

            g.memset(proj[:, :], 0.0).then_inc(proj_zero, 1)
            g.wait_ge(ids_ok, 3)
            gather(0)
            n = 0
            for t_, v_ in ((consts[:, 0:1], -0.5), (consts[:, 1:2], EMB_EPS), (consts[:, 2:3], LN_EPS),
                           (halves[:, :], 0.5), (ones[:, :], 1.0), (ident[:, :], 0.0),
                           (half_sq[:, :, :], 0.125), (mask_f[:, :, :], 0.0), (pair_mask[:, :, :], 1.0)):
                g.memset(t_, v_).then_inc(g_const, 1)
            g.iota(iota_i[:, :], pattern=[[1, PROTO]], base=0, channel_multiplier=0).then_inc(g_const, 1)
            g.wait_ge(g_const, 10)
            g.affine_select(out=ident[:, :], in_=ident[:, :], compare_op=ALU.not_equal, fill=1.0, base=0,
                            pattern=[[-1, P]], channel_multiplier=1).then_inc(g_const, 1)
            g.affine_select(out=half_sq[:, :, :], in_=half_sq[:, :, :], compare_op=ALU.is_ge, fill=0.0, base=0,
                            pattern=[[P, KC], [-DH, H]], channel_multiplier=1).then_inc(g_const, 1)
            g.affine_select(out=mask_f[:, 0, :], in_=mask_f[:, 0, :], compare_op=ALU.is_ge, fill=HIDDEN_SCORE,
                            base=0, pattern=[[-1, P]], channel_multiplier=1).then_inc(g_const, 1)
            g.affine_select(out=mask_f[:, 1, :], in_=mask_f[:, 1, :], compare_op=ALU.is_ge, fill=HIDDEN_SCORE,
                            base=0, pattern=[[1, P]], channel_multiplier=-1).then_inc(g_const, 1)
            g.affine_select(out=pair_mask[:, :, 0:VA], in_=pair_mask[:, :, 0:VA], compare_op=ALU.is_ge, fill=0.0,
                            base=M - 1, pattern=[[0, HP], [0, VA]], channel_multiplier=-1).then_inc(g_const, 1)
            g.affine_select(out=pair_mask[:, :, VA:], in_=pair_mask[:, :, VA:], compare_op=ALU.is_ge, fill=0.0,
                            base=-M, pattern=[[0, HP], [0, VA]], channel_multiplier=1).then_inc(g_const, 1)
            g.wait_ge(g_const, 16)
            g.affine_select(out=half_sq[:, :, :], in_=half_sq[:, :, :], compare_op=ALU.is_ge, fill=0.0, base=DH - 1,
                            pattern=[[-P, KC], [DH, H]], channel_multiplier=-1).then_inc(g_const, 1)
            g.wait_ge(load["E"], 16 * N_LOAD["E"])

            def ln_power(x, t, eps_col):
                wait(g, ln_v[x], 3 * t + 2)
                g.tensor_tensor(rstd[x][:, 0:1], mv[x][:, 1:2], consts[:, eps_col:eps_col + 1], ALU.add)\
                    .then_inc(ln_g[x], 1)
                wait(g, ln_g[x], 2 * t + 1)
                g.tensor_tensor(rstd[x][:, 1:2], rstd[x][:, 0:1], consts[:, 0:1], ALU.pow).then_inc(ln_g[x], 1)

            def step(s):
                if s.has("R"):
                    t = s.tile("R")
                    wait(g, rope_ok, 3 * t + 3)
                    wait(g, rothi_ok, 3 * t)
                    g.tensor_tensor(rot[:, :, :].rearrange("p h d -> p (h d)"), rc[:, :], rs[:, :], ALU.add)\
                        .then_inc(rot_ok, 1)
                if s.has("E"):
                    t = s.tile("E")
                    wait(g, gathered, 48 * t + 48)
                    g.tensor_tensor(esum1[:, :], emb[:, 0, :], emb[:, 1, :], ALU.add).then_inc(e_sum, 1)
                    wait(g, e_sum, 2 * t + 1)
                    g.tensor_tensor(esum[:, :], esum1[:, :], emb[:, 2, :], ALU.add).then_inc(e_sum, 1)
                if s.has("R"):
                    t = s.tile("R")
                    wait(g, rothi_ok, 3 * t + 1)
                    g.tensor_tensor(slots(32), rot[:, :, :], slots(16), ALU.subtract).then_inc(rotlo_ok, 1)
                if s.has("M"):
                    t = s.tile("M")
                    if s.static and t == 0:
                        g.wait_ge(load["M"], 16 * N_LOAD["M"])
                    wait(g, hR_ok, t + 1)
                    wait(g, out_ok, t)
                    g.tensor_tensor(hb[:, :], h_of(t), b2[:, :], ALU.add).then_inc(hb_ok, 1)
                    wait(g, mh_ok, 2 * t + 2)
                    wait(g, y2_ps, t)
                    g.tensor_tensor(mlo[:, :, :], mh[:, :, :], mhi[:, :, :], ALU.subtract).then_inc(mlo_ok, 1)
                if s.has("F"):
                    t = s.tile("F")
                    wait(g, near_ok, t + 1)
                    g.tensor_tensor(dist[:, :], near[:, :], halves[:, :], ALU.pow).then_inc(dist_ok, 1)
                if s.has("E"):
                    t = s.tile("E")
                    ln_power("E", t, 1)
                    wait(g, ln_v["E"], 3 * t + 3)
                    g.tensor_tensor(escaled[:, :], ehat[:, :], gamma[:, :], ALU.mult).then_inc(e_out, 1)
                    wait(g, e_out, 2 * t + 1)
                    g.tensor_tensor(h_of(t), escaled[:, :], beta[:, :], ALU.add).then_inc(e_out, 1)
                if s.has("E"):
                    t = s.tile("E")
                    if s.first:
                        ln_power("P", t, 2)
                    if s.next_gather():
                        gather(t + 1)
                    if not s.first:
                        ln_power("P", t, 2)
                if s.has("F"):
                    ln_power("R", s.tile("F"), 2)
                if s.has("P"):
                    ln_power("F", s.tile("P"), 2)
                if s.has("R"):
                    ln_power("M", s.tile("R"), 2)

            for i in range(FIRST_STEP, LOOP_FROM):
                step(Step(i))
            with g.Fori(LOOP_FROM, LOOP_TO) as i:
                step(Step(i))
            for i in range(LOOP_TO, LAST_STEP + 1):
                step(Step(i))

        @block.vector
        def _(v):
            def held(sem_, count):
                wait(v, sem_, count)
                v.sem_inc(v_held, 1)

            def bc(ap, shape):
                return ap.to_broadcast(shape)

            v.wait_ge(ids_in, 16)
            for k, n in enumerate((VOCAB, POS, TYPES)):
                v.tensor_scalar(ids_neg[:, k, :], ids[:, k, :], 0.0, float(n), ALU.is_lt, ALU.mult).then_inc(v_const, 1)
            for k in range(3):
                v.wait_ge(v_const, k + 1)
                v.tensor_tensor(ids[:, k, :], ids[:, k, :], ids_neg[:, k, :], ALU.add).then_inc(v_const, 1)
            for k, n in enumerate((VOCAB, POS, TYPES)):
                v.wait_ge(v_const, 4 + k)
                v.tensor_scalar(ids[:, k, :], ids[:, k, :], 0.0, float(n - 1), ALU.max, ALU.min).then_inc(ids_ok, 1)

            def norm_sums(x, t, src, sem_, count):
                held(sem_, count)
                v.bn_stats(stats[x][:, :], src).then_inc(ln_v[x], 1)

            def norm_join(x, t):
                held(ln_v[x], 3 * t + 1)
                v.bn_aggr(mv[x][:, :], stats[x][:, :]).then_inc(ln_v[x], 1)

            def norm_stats(x, t, src, sem_, count):
                norm_sums(x, t, src, sem_, count)
                norm_join(x, t)

            def norm_apply(x, t, src, dst):
                wait(v, ln_g[x], 2 * t + 2)
                v.tensor_scalar(dst, src, mv[x][:, 0:1], rstd[x][:, 1:2], ALU.subtract, ALU.mult)\
                    .then_inc(ln_v[x], 1)

            def td(bank):
                return PS[:, bank:bank + 2, 0:8 * M].rearrange("p b (h m) -> p b h m", m=M)

            def heads(tile_):
                return tile_[:, :].rearrange("p (b h m) -> p b h m", b=2, m=M)

            def per_head(ap):
                return bc(ap.rearrange("p (b h) -> p b h", b=2).unsqueeze(3), [P, 2, 8, M])

            def setup_p():
                v.wait_ge(proj_in, 16 * 8)
                v.tensor_scalar(proj[:, :], proj[:, :], 0.5, None, ALU.mult).then_inc(s_const, 1)
                v.memset(va[:, :, :], 1.0).then_inc(s_const, 1)
                v.wait_ge(s_const, 2)
                v.wait_ge(wof_ps, 3)
                v.tensor_copy(wof[:, :, :], PS[:, 4:6, 0:D]).then_inc(wof_ok, 1)
                v.wait_ge(load["P"], 16 * N_LOAD["P"])
                v.tensor_tensor(bof[:, :], PS[:, 6, 0:D], bfc[:, :], ALU.add).then_inc(wof_ok, 1)
                v.wait_ge(wof_ok, 2)

            def split_weights(name, n):
                v.wait_ge(whi_ok, n)
                v.scalar_tensor_tensor(out=wlo[name][:, :, :], in0=SPLITS[name][0][:, :, :], scalar=WS,
                                       in1=whi[name][:, :, :], op0=ALU.mult, op1=ALU.subtract).then_inc(wlo_ok, 1)

            def setup_f():
                v.wait_ge(load["F"], 16 * N_LOAD["F"])
                v.tensor_tensor(proto_sq[:, :, :], protoT[:, :, :], protoT[:, :, :], ALU.mult).then_inc(p2_ok, 1)
                v.tensor_scalar(protoT2[:, :, :], protoT[:, :, :], 2.0, None, ALU.mult).then_inc(p2_ok, 1)
                v.wait_ge(g_const, 17)
                v.tensor_copy(iota[:, :], iota_i[:, :]).then_inc(p2_ok, 1)
                v.tensor_scalar(temp[:, 1:2], temp[:, 0:1], -1.0, None, ALU.mult).then_inc(p2_ok, 1)
                v.wait_ge(p2_ok, 4)
                v.tensor_tensor(temp[:, 2:3], temp[:, 0:1], temp[:, 1:2], ALU.max).then_inc(p2_ok, 1)
                v.wait_ge(p2_ok, 5)
                v.tensor_scalar(temp[:, 3:4], temp[:, 2:3], 0.1, -WS ** 0.5, ALU.max, ALU.mult).then_inc(p2_ok, 1)
                v.wait_ge(p2_ok, 6)
                v.reciprocal(temp[:, 2:3], temp[:, 3:4]).then_inc(p2_ok, 1)
                v.wait_ge(p2_ok, 7)
                v.wait_ge(p2_ps, 1)
                v.tensor_scalar(p2[:, :], PS[0:1, 6, 0:PROTO], -WS, None, ALU.mult).then_inc(p2_ok, 1)
                split_weights("fbT", 3)
                split_weights("protoT2", 4)

            def setup_constants():
                v.memset(split[:, :], 0.0).then_inc(tern_abs, 1)
                v.memset(vhi[:, :, :], 1.0).then_inc(tern_abs, 1)
                v.memset(vlo[:, :, :], 0.0).then_inc(tern_abs, 1)

            def setup_masks():
                v.wait_ge(g_const, 17)
                v.tensor_copy(ident_b[:, :], ident[:, :]).then_inc(tern_abs, 1)
                v.tensor_copy(ident_h[:, :], ident[:, :]).then_inc(tern_abs, 1)
                v.tensor_copy(head_row[:, :, :], bc(ident[0:H, 0:H].unsqueeze(2), [H, H, P])).then_inc(tern_abs, 1)
                v.tensor_copy(mask_qk[:, :, :], bc(mask_f[:, 0:1, :], [P, 4, P])).then_inc(tern_abs, 1)
                v.tensor_copy(mask_kq[:, :, :], bc(mask_f[:, 1:2, :], [P, 4, P])).then_inc(tern_abs, 1)

            def setup_r():
                v.wait_ge(load["R"], 16 * N_LOAD["R"])
                for table in (rope_cos, rope_sin):
                    v.tensor_scalar(table[:, 0:D], table[:, 0:D], 0.25 / WS, None, ALU.mult).then_inc(tern_abs, 1)
                    v.tensor_scalar(table[:, D:], table[:, D:], 1.0 / WS, None, ALU.mult).then_inc(tern_abs, 1)

            def abs_sum(k, w):
                v.wait_ge(load["M"], 16 * N_LOAD["M"])
                v.tensor_reduce(absum[:, k:k + 1], w[:, :], AX_X, ALU.add, apply_absolute_value=True)\
                    .then_inc(tern_abs, 1)

            def thresholds():
                v.wait_ge(tern_ps, 1)
                v.tensor_scalar(thr[:, 0:2], PS[:, 6, 0:2], 1.0 / (D * F1), QUANT_EPS, ALU.mult, ALU.add)\
                    .then_inc(tern, 1)
                v.wait_ge(tern, 1)
                v.tensor_scalar(thr[:, 2:4], thr[:, 0:2], -0.5, None, ALU.mult).then_inc(tern, 1)
                v.wait_ge(tern, 2)
                v.tensor_scalar(thr[:, 0:2], thr[:, 0:2], 0.5, None, ALU.mult).then_inc(tern, 1)
                v.wait_ge(tern, 3)

            def quantise(k, half):
                w, q = ((w1, w1q), (w2, w2q))[k]
                o, n = half * F1, 3 + 4 * k + 2 * half
                v.wait_ge(tern, n)
                v.tensor_scalar(wneg[:, :], w[:, o:o + F1], thr[:, 2 + k:3 + k], None, ALU.is_lt).then_inc(tern, 1)
                v.wait_ge(tern, n + 1)
                v.scalar_tensor_tensor(out=q[:, :, :].rearrange("p c n -> p (c n)")[:, o:o + F1], in0=w[:, o:o + F1],
                                       scalar=thr[:, k:k + 1], in1=wneg[:, :], op0=ALU.is_gt, op1=ALU.subtract)\
                    .then_inc(tern, 1)

            def setup_between(step_, place):
                if step_ == 1:
                    if place == 0:
                        setup_r()
                    elif place == 1:
                        split_weights("rwqk", 5)
                    elif place == 2:
                        split_weights("rwv", 6)
                    else:
                        abs_sum(place - 3, (w1, w2)[place - 3])
                elif step_ == 2 and place != 2:
                    quantise(*{0: (0, 0), 1: (0, 1), 3: (1, 0), 4: (1, 1)}[place])

            def x_lo(x, t, bank):
                wait(v, xT_ok[x], t + 1)
                v.tensor_tensor(xlo[x][:, :, :], PS[:, bank, 0:D].rearrange("p (c n) -> p c n", c=KC),
                                xhi[x][:, :, :], ALU.subtract).then_inc(xlo_ok[x], 1)

            def by_head(ap):
                return ap.rearrange("p (h d) -> p h d", d=DH)

            def step(s):
                if s.has("M"):
                    t = s.tile("M")
                    wait(v, xT_ps["M"], t)
                    norm_apply("M", t, h_of(t), xn["M"][:, :])
                if s.has("P"):
                    t = s.tile("P")
                    wait(v, qk_ps, t + 1)
                    wait(v, sq_ok, t)
                    wait(v, tdq_ps, t)
                    v.scalar_tensor_tensor(out=qkT[:, :, :], in0=PS[:, 7, :].rearrange("p (c n) -> p c n", c=4),
                                           scalar=1.0 / WS, in1=bc(bqk[:, :].unsqueeze(2), [P, 4, P]),
                                           op0=ALU.mult, op1=ALU.add).then_inc(qk_ok, 1)
                if s.has("R"):
                    t = s.tile("R")
                    wait(v, rqk_ps, t + 1)
                    wait(v, rot_ok, t)
                    v.tensor_tensor(rc[:, :], PS[:, 4, :], rope_cos[:, :], ALU.mult).then_inc(rope_ok, 1)
                if s.has("M"):
                    x_lo("M", s.tile("M"), 1)
                if s.has("R"):
                    x = PS[:, 4, :].rearrange("p (n two) -> p n two", two=2)
                    y = rs[:, :].rearrange("p (n two) -> p n two", two=2)
                    z = rope_sin[:, :].rearrange("p (n two) -> p n two", two=2)
                    v.tensor_tensor(y[:, :, 0], x[:, :, 1], z[:, :, 0], ALU.mult).then_inc(rope_ok, 1)
                    v.tensor_tensor(y[:, :, 1], x[:, :, 0], z[:, :, 1], ALU.mult).then_inc(rope_ok, 1)
                if s.has("F"):
                    x_lo("F", s.tile("F"), 5)
                if s.has("R"):
                    t = s.tile("R")
                    wait(v, vhi_ok, t + 1)
                    wait(v, pv_ps, t)
                    v.scalar_tensor_tensor(out=vlo[:, :, 0:DH], in0=by_head(PS[:, 0, 0:D]), scalar=1.0 / WS,
                                           in1=vhi[:, :, 0:DH], op0=ALU.mult, op1=ALU.subtract).then_inc(vlo_ok, 1)
                if s.has("P"):
                    t = s.tile("P")
                    wait(v, v_ps, t + 1)
                    wait(v, ctx_ps, t)
                    v.scalar_tensor_tensor(out=va[:, :, 0:DH], in0=by_head(PS[:, 7, 0:D]), scalar=1.0 / WS,
                                           in1=by_head(bv[:, :]), op0=ALU.mult, op1=ALU.add).then_inc(v_ok, 1)
                if s.static:
                    setup_between(s.i, 0)
                if s.has("P"):
                    t = s.tile("P")
                    wait(v, tdk_ps, t + 1)
                    v.tensor_reduce(kmx[:, :].rearrange("p (b h) -> p b h", b=2), td(4), AX_X, ALU.max)\
                        .then_inc(kmx_ok, 1)
                if s.static:
                    setup_between(s.i, 1)
                if s.has("E"):
                    t = s.tile("E")
                    norm_stats("E", t, esum[:, :], e_sum, 2 * t + 2)
                if s.has("P"):
                    t = s.tile("P")
                    wait(v, kmxT_ps, t + 1)
                    v.tensor_reduce(kmx_row[:, :], PS[0:H, 6, 0:P], AX_X, ALU.max).then_inc(kdiag_ok, 1)
                    wait(v, kdiag_ok, 2 * t + 1)
                    v.tensor_scalar(kdiag[:, :], ident[0:H, 0:H], kmx_row[:, 0:1], None, ALU.mult)\
                        .then_inc(kdiag_ok, 1)
                if s.has("F"):
                    t = s.tile("F")
                    wait(v, proto_ps, t + 1)
                    wait(v, x2_ok, t + 1)
                    v.tensor_scalar(nd2[:, :], PS[:, 6, 0:PROTO], x2[:, 0:1], 0.0, ALU.subtract, ALU.min)\
                        .then_inc(d2_ok, 1)
                if s.has("R"):
                    t = s.tile("R")
                    wait(v, rT_ps, t + 1)
                    wait(v, s2_ps, t)
                    v.tensor_copy(rT[:, 0:HP, :].rearrange("p c n -> p (c n)"), PS[:, 0, :].bitcast(F16))\
                        .then_inc(rqT_ok, 1)
                if s.has("F"):
                    t = s.tile("F")
                    held(d2_ok, t + 1)
                    v.max(top[:, :], nd2[:, :]).then_inc(gap_ok, 1)
                    wait(v, gap_ok, 4 * t + 1)
                    v.tensor_scalar(near[:, :], top[:, 0:2], -1.0, None, ALU.mult).then_inc(near_ok, 1)
                    held(near_ok, t + 1)
                    v.max_index(topi[:, :], top[:, :], nd2[:, :]).then_inc(gap_ok, 1)
                    wait(v, gap_ok, 4 * t + 2)
                    v.tensor_copy(topf[:, :], topi[:, 0:2]).then_inc(gap_ok, 1)
                if s.has("P"):
                    t = s.tile("P")
                    wait(v, kb_ok, t + 1)
                    wait(v, ke_ok, t)
                    v.tensor_tensor(heads(kd), td(4), per_head(kb[:, 0:H]), ALU.subtract).then_inc(kd_ok, 1)
                if s.static:
                    setup_between(s.i, 2)
                if s.has("R"):
                    t = s.tile("R")
                    wait(v, s1_ps, t + 1)
                    wait(v, nmT_ps, t)
                    v.tensor_reduce(negmax[:, :].rearrange("p (c j) -> p j c", j=4),
                                    PS[:, 0:4, :].rearrange("p j (c k) -> p j c k", c=4), AX_X, ALU.max,
                                    negate=True).then_inc(rmax_ok, 1)
                if s.has("E"):
                    t = s.tile("E")
                    norm_apply("E", t, esum[:, :], ehat[:, :])
                if s.has("F"):
                    t = s.tile("F")
                    wait(v, dist_ok, t + 1)
                    v.tensor_scalar(gap[:, :], dist[:, 1:2], dist[:, 0:1], temp[:, 2:3], ALU.subtract, ALU.mult)\
                        .then_inc(gap_ok, 1)
                if s.has("P"):
                    t = s.tile("P")
                    wait(v, tdq_ps, t + 1)
                    v.tensor_reduce(qmx[:, :].rearrange("p (b h) -> p b h", b=2), td(4), AX_X, ALU.max)\
                        .then_inc(qb_ok, 1)
                    wait(v, qb_ok, 2 * t + 1)
                    v.tensor_tensor(qb[:, :], qmx[:, :], kb[:, H:], ALU.add).then_inc(qb_ok, 1)
                    wait(v, qb_ok, 2 * t + 2)
                    wait(v, qe_ok, t)
                    v.tensor_tensor(heads(qd), td(4), per_head(qb[:, :]), ALU.subtract).then_inc(qd_ok, 1)
                if s.static:
                    setup_between(s.i, 3)
                if s.has("F"):
                    t = s.tile("F")
                    wait(v, gap_ok, 4 * t + 3)
                    wait(v, second_ok, t + 1)
                    wait(v, hF_ok, t)
                    v.tensor_scalar(wsum[:, 0:1], second[:, :], 1.0, None, ALU.add).then_inc(gate_ok, 1)
                    v.tensor_scalar(gate1[:, :], iota[:, :], topf[:, 1:2], second[:, 0:1], ALU.is_equal, ALU.mult)\
                        .then_inc(gate_ok, 1)
                    wait(v, gate_ok, 4 * t + 2)
                    v.reciprocal(wsum[:, 1:2], wsum[:, 0:1]).then_inc(gate_ok, 1)
                    wait(v, hgT_ps, 2 * t)
                    v.scalar_tensor_tensor(out=hg[:, R2:], in0=iota[:, :], scalar=topf[:, 0:1], in1=gate1[:, :],
                                           op0=ALU.is_equal, op1=ALU.add).then_inc(gate_ok, 1)
                    wait(v, gate_ok, 4 * t + 4)
                    wait(v, fh_ps, t + 1)
                    v.scalar_tensor_tensor(out=hg[:, 0:R2].rearrange("p (e r) -> p e r", r=RANK),
                                           in0=PS[:, 7, :].rearrange("p (e r) -> p e r", r=RANK), scalar=1.0 / WS,
                                           in1=bc(hg[:, R2:].unsqueeze(2), [P, PROTO, RANK]), op0=ALU.mult,
                                           op1=ALU.mult).then_inc(hg_ok, 1)
                if s.has("M"):
                    t = s.tile("M")
                    wait(v, y2_ps, t + 1)
                    wait(v, hb_ok, t + 1)
                    wait(v, stored, 16 * t)
                    v.tensor_tensor(outb[:, :], PS[:, 6, 0:D], hb[:, :], ALU.add).then_inc(out_ok, 1)
                if s.has("E"):
                    t = s.tile("E")
                    norm_stats("P", t, h_of(t), e_out, 2 * t + 2)
                if s.has("F"):
                    t = s.tile("F")
                    wait(v, hgT_ps, 2 * t + 1)
                    wait(v, y_ps, t)
                    v.tensor_copy(hgT[:, :, :], PS[:, 7, :].rearrange("p (c n) -> p c n", c=4)).then_inc(hgT_ok, 1)
                if s.has("E"):
                    t = s.tile("E")
                    wait(v, xT_ps["P"], t)
                    norm_apply("P", t, h_of(t), xn["P"][:, :])
                if s.has("P"):
                    t = s.tile("P")
                    wait(v, ctx_ps, t + 1)
                    wait(v, o_ps, t)
                    v.tensor_tensor(ctxt[:, :, :], PS[0:MP, 6, 0:H * VA].rearrange("p (a b) -> p a b", a=HP),
                                    pair_mask[:, :, :], ALU.mult).then_inc(ctx_ok, 1)
                if s.static:
                    setup_between(s.i, 4)
                if s.has("R"):
                    t = s.tile("R")
                    wait(v, phi_ok, 4 * t + 2)
                    wait(v, pv_ps, t)
                    v.tensor_tensor(plo[:, 0:2, :, :], pfull[:, 0:2, :, :], phi[:, 0:2, :, :],
                                    ALU.subtract).then_inc(plo_ok, 1)
                if s.has("F"):
                    t = s.tile("F")
                    wait(v, hgT_ps, 2 * t + 2)
                    v.tensor_copy(gT[:, :], PS[0:PROTO, 6, 0:P]).then_inc(hgT_ok, 1)
                if s.has("R"):
                    t = s.tile("R")
                    wait(v, phi_ok, 4 * t + 4)
                    wait(v, pv_ps, t)
                    v.tensor_tensor(plo[:, 2:4, :, :], pfull[:, 2:4, :, :], phi[:, 2:4, :, :],
                                    ALU.subtract).then_inc(plo_ok, 1)
                if s.has("P"):
                    t = s.tile("P")
                    wait(v, o_ps, t + 1)
                    o = PS[:, 4, 0:H * VA].rearrange("p (h d) -> p h d", d=VA)
                    v.reciprocal(oden[:, :], o[:, :, DH]).then_inc(o_ok, 1)
                    wait(v, o_ok, 2 * t + 1)
                    wait(v, oT_ps, t)
                    v.tensor_tensor(by_head(onorm[:, :]), o[:, :, 0:DH], bc(oden[:, :].unsqueeze(2), [P, H, DH]),
                                    ALU.mult).then_inc(o_ok, 1)
                if s.has("F"):
                    t = s.tile("F")
                    wait(v, y_ps, t + 1)
                    v.scalar_tensor_tensor(out=h_of(t), in0=PS[:, 7, 0:D], scalar=wsum[:, 1:2], in1=h_of(t),
                                           op0=ALU.mult, op1=ALU.add).then_inc(hF_ok, 1)
                if s.has("R"):
                    t = s.tile("R")
                    wait(v, pv_ps, t + 1)
                    o = PS[:, 5, 0:H * VA].rearrange("p (h d) -> p h d", d=VA)
                    v.reciprocal(rden[:, :], o[:, :, DH]).then_inc(ro_ok, 1)
                    wait(v, ro_ok, 2 * t + 1)
                    wait(v, roT_ps, t)
                    v.tensor_tensor(by_head(rout[:, :]), o[:, :, 0:DH], bc(rden[:, :].unsqueeze(2), [P, H, DH]),
                                    ALU.mult).then_inc(ro_ok, 1)
                if s.has("F"):
                    t = s.tile("F")
                    norm_stats("R", t, h_of(t), hF_ok, t + 1)
                if s.has("F"):
                    t = s.tile("F")
                    wait(v, xT_ps["R"], t)
                    norm_apply("R", t, h_of(t), xn["R"][:, :])
                if s.has("E"):
                    t = s.tile("E")
                    wait(v, v_ps, t)
                    x_lo("P", t, 0)
                if s.has("P"):
                    t = s.tile("P")
                    wait(v, of_ps, t + 1)
                    v.tensor_tensor(ofb[:, :], PS[:, 6, 0:D], bof[:, :], ALU.add).then_inc(hP_ok, 1)
                    wait(v, hP_ok, 2 * t + 1)
                    v.scalar_tensor_tensor(out=h_of(t), in0=ofb[:, :], scalar=0.0, in1=h_of(t),
                                           op0=ALU.max, op1=ALU.add).then_inc(hP_ok, 1)
                if s.has("F"):
                    t = s.tile("F")
                    wait(v, rv_ps, t)
                    x_lo("R", t, 1)
                if s.has("R"):
                    t = s.tile("R")
                    wait(v, wo_ps, t + 1)
                    v.tensor_tensor(h_of(t), PS[:, 5, 0:D], h_of(t), ALU.add).then_inc(hR_ok, 1)
                if s.has("P"):
                    t = s.tile("P")
                    norm_sums("F", t, h_of(t), hP_ok, 2 * t + 2)
                if s.has("R"):
                    t = s.tile("R")
                    norm_sums("M", t, h_of(t), hR_ok, t + 1)
                if s.has("P"):
                    norm_join("F", s.tile("P"))
                if s.has("R"):
                    norm_join("M", s.tile("R"))
                if s.has("P"):
                    t = s.tile("P")
                    wait(v, xT_ps["F"], t)
                    wait(v, x2_ok, t)
                    norm_apply("F", t, h_of(t), xn["F"][:, :])

            setup_constants()
            v.wait_ge(load["P"], 16 * N_LOAD["P"])
            split_weights("wqkT", 1)
            split_weights("wvT", 2)
            step(Step(-1))
            setup_p()
            setup_masks()
            step(Step(0))
            setup_f()
            step(Step(1))
            thresholds()
            for i in range(2, LOOP_FROM):
                step(Step(i))
            with v.Fori(LOOP_FROM, LOOP_TO) as i:
                step(Step(i))
            for i in range(LOOP_TO, LAST_STEP + 1):
                step(Step(i))

        @block.scalar
        def _(a):
            def copy(dst, src, bias=0.0):
                return a.activation(dst, src, ACT.Identity if bias else ACT.Copy, bias=bias)

            def x_hi(x, t, bank, reader):
                wait(a, xT_ps[x], t + 1)
                wait(a, reader, t)
                copy(xhi[x][:, :, :], PS[:, bank, 0:D].rearrange("p (c n) -> p c n", c=KC)).then_inc(xT_ok[x], 1)

            def split_weights(name):
                a.activation(whi[name][:, :, :], SPLITS[name][0][:, :, :], ACT.Copy, scale=WS).then_inc(whi_ok, 1)

            def step(s):
                if s.has("F"):
                    x_hi("F", s.tile("F"), 5, proto_ps)
                if s.has("R"):
                    t = s.tile("R")
                    wait(a, rv_ps, t + 1)
                    wait(a, pv_ps, t)
                    if s.static:
                        a.wait_ge(tern_abs, 2)
                    a.activation(vhi[:, :, 0:DH], PS[:, 0, 0:D].rearrange("p (h d) -> p h d", d=DH), ACT.Copy,
                                 scale=1.0 / WS).then_inc(vhi_ok, 1)
                if s.has("M"):
                    x_hi("M", s.tile("M"), 1, m_ps)
                if s.has("P"):
                    t = s.tile("P")
                    wait(a, qk_ok, t + 1)
                    wait(a, kb_ps, t)
                    a.activation(sqT[:, :, :], qkT[:, :, :], ACT.Square).then_inc(sq_ok, 1)
                if s.has("R"):
                    t = s.tile("R")
                    wait(a, rot_ok, t + 1)
                    wait(a, rT_ps, t)
                    wait(a, rotlo_ok, t)
                    copy(slots(16), rot[:, :, :]).then_inc(rothi_ok, 1)
                    copy(slots(0)[:, 0:H, :], rot[:, 0:H, :]).then_inc(rothi_ok, 1)
                    copy(slots(48)[:, H:, :], rot[:, H:, :]).then_inc(rothi_ok, 1)
                if s.has("F"):
                    t = s.tile("F")
                    wait(a, ln_v["F"], 3 * t + 3)
                    wait(a, d2_ok, t)
                    a.activation(xsq[:, :], xn["F"][:, :], ACT.Square, scale=WS ** 0.5, accum_out=x2[:, 0:1])\
                        .then_inc(x2_ok, 1)
                if s.has("M"):
                    t = s.tile("M")
                    wait(a, m_ps, t + 1)
                    wait(a, mlo_ok, t)
                    for m in range(FC):
                        last = a.activation(mh[:, m, :], PS[:, 2 + m // 4, m % 4 * P:(m % 4 + 1) * P], ACT.Relu,
                                            bias=b1[:, m:m + 1])
                    last.then_inc(mh_ok, 1)
                    wait(a, mh_ok, 2 * t + 1)
                    wait(a, y2_ps, t)
                    copy(mhi[:, :, :], mh[:, :, :]).then_inc(mh_ok, 1)
                if s.has("R"):
                    t = s.tile("R")
                    wait(a, rT_ps, t + 1)
                    wait(a, s2_ps, t)
                    copy(rT[:, HP:, :].rearrange("p c n -> p (c n)"), PS[:, 1, :].bitcast(F16)).then_inc(rkT_ok, 1)
                if s.has("P"):
                    t = s.tile("P")
                    wait(a, kb_ps, t + 1)
                    wait(a, qb_ok, 2 * t)
                    wait(a, kd_ok, t)
                    copy(kb[:, :], PS[:, 6, 0:2 * H]).then_inc(kb_ok, 1)
                    wait(a, kd_ok, t + 1)
                    wait(a, kp_ok, t)
                    a.activation(ke[:, :], kd[:, :], ACT.Exp).then_inc(ke_ok, 1)
                    wait(a, ke_ok, t + 1)
                    wait(a, ctx_ps, t)
                    copy(kp[:, :], ke[:, :], FEATURE_EPS).then_inc(kp_ok, 1)
                if s.has("R"):
                    t = s.tile("R")
                    wait(a, nmT_ps, t + 1)
                    wait(a, s2_ps, t)
                    copy(negmaxT[:, :], PS[0:H, 0, 0:P // 2].bitcast(F16)).then_inc(nmT_ok, 1)
                if s.has("F"):
                    t = s.tile("F")
                    wait(a, gap_ok, 4 * t + 4)
                    wait(a, gate_ok, 4 * t)
                    a.activation(second[:, :], gap[:, :], ACT.Exp).then_inc(second_ok, 1)
                if s.has("P"):
                    t = s.tile("P")
                    wait(a, qd_ok, t + 1)
                    wait(a, qp_ps, t)
                    a.activation(qe[:, :], qd[:, :], ACT.Exp).then_inc(qe_ok, 1)
                if s.has("R"):
                    t = s.tile("R")
                    wait(a, s2_ps, t + 1)
                    wait(a, pv_ps, t)
                    wait(a, plo_ok, 2 * t)
                    for b in (0, 2):
                        for dst in (phi, pfull):
                            a.activation(dst[:, b:b + 2, :, :],
                                         PS[:, b:b + 2, :].rearrange("p j (c q) -> p j c q", c=4), ACT.Exp)\
                                .then_inc(phi_ok, 1)
                if s.has("P"):
                    t = s.tile("P")
                    wait(a, qp_ps, t + 1)
                    wait(a, o_ps, t)
                    copy(qp[:, :, :], PS[0:MP, 4:6, :].rearrange("p b (c n) -> p (b c) n", c=4), FEATURE_EPS)\
                        .then_inc(qp_ok, 1)
                if s.has("P"):
                    t = s.tile("P")
                    wait(a, oT_ps, t + 1)
                    wait(a, of_ps, t)
                    copy(oT[:, :, :], PS[:, 1, 0:D].rearrange("p (c n) -> p c n", c=KC)).then_inc(oT_ok, 1)
                if s.has("E"):
                    x_hi("P", s.tile("E"), 0, v_ps)
                if s.has("R"):
                    t = s.tile("R")
                    wait(a, roT_ps, t + 1)
                    wait(a, wo_ps, t)
                    copy(roT[:, :, :], PS[:, 4, 0:D].rearrange("p (c n) -> p c n", c=KC)).then_inc(roT_ok, 1)
                if s.has("F"):
                    x_hi("R", s.tile("F"), 1, rv_ps)

            a.wait_ge(load["P"], 16 * N_LOAD["P"])
            split_weights("wqkT")
            split_weights("wvT")
            step(Step(-1))
            a.wait_ge(load["F"], 16 * N_LOAD["F"])
            split_weights("fbT")
            step(Step(0))
            a.wait_ge(p2_ok, 2)
            split_weights("protoT2")
            a.wait_ge(load["R"], 16 * N_LOAD["R"])
            split_weights("rwqk")
            split_weights("rwv")
            step(Step(1))
            a.wait_ge(load["M"], 16 * N_LOAD["M"])
            for i in range(2, LOOP_FROM):
                step(Step(i))
            with a.Fori(LOOP_FROM, LOOP_TO) as i:
                step(Step(i))
            for i in range(LOOP_TO, LAST_STEP + 1):
                step(Step(i))

        @block.tensor
        def _(pe):
            def transpose2(bank, x):
                for c in range(KC):
                    last = pe.transpose(PS[:, bank, c * P:(c + 1) * P], x[:, c * P:(c + 1) * P], ident[:, :])
                return last

            def token_major(dst, x, w):
                for c in range(KC):
                    last = pe.matmul(dst, x[:, c, :], w[:, c, :], start=(c == 0), stop=(c == KC - 1))
                return last

            def split_product(dst, x, w, first=True, last_=True):
                n = 0
                for c in range(KC):
                    for xp, wp in ((xhi, whi), (xhi, wlo), (xlo, whi)):
                        last = pe.matmul(dst, xp[x][:, c, :], wp[w][:, c, :], start=(first and n == 0),
                                         stop=(last_ and n == 3 * KC - 1))
                        n += 1
                return last

            def masks(banks, mask):
                for j in banks:
                    pe.matmul(PS[:, j, :], ident_b[:, :], mask[:, :, :].rearrange("p c k -> p (c k)"),
                              start=True, stop=False, skip_group_check=True)

            def features(bank, c0):
                for c in range(KC):
                    last = pe.matmul(PS[:, bank + c, 0:8 * M], qkT[:, c0 + c, :], proj[:, :], start=True, stop=True)
                return last

            def step(s):
                E_, P_, F_, R_, M_ = (s.has(x) for x in "EPFRM")
                e, p, f, r, m = (s.tile(x) for x in "EPFRM")
                if P_:
                    wait(pe, xT_ok["P"], p + 1)
                    wait(pe, xlo_ok["P"], p + 1)
                    wait(pe, oT_ok, p)
                    wait(pe, hF_ok, s.before("F"))
                    for j in range(4):
                        n = 0
                        for c in range(KC):
                            for xp, wp in ((xhi, whi), (xlo, whi), (xhi, wlo)):
                                last = pe.matmul(PS[:, 7, j * P:(j + 1) * P], wp["wqkT"][:, c, j * P:(j + 1) * P],
                                                 xp["P"][:, c, :], start=(n == 0), stop=(n == 3 * KC - 1))
                                n += 1
                    last.then_inc(qk_ps, 1)
                if R_:
                    wait(pe, xT_ok["R"], r + 1)
                    wait(pe, xlo_ok["R"], r + 1)
                    wait(pe, roT_ok, r)
                    wait(pe, o_ok, 2 * s.before("P"))
                    split_product(PS[:, 4, :], "R", "rwqk").then_inc(rqk_ps, 1)
                if F_:
                    wait(pe, ln_v["F"], 3 * f + 3)
                    wait(pe, hR_ok, s.before("R"))
                    transpose2(5, xn["F"]).then_inc(xT_ps["F"], 1)
                if R_:
                    wait(pe, xlo_ok["P"], s.before("E"))
                    wait(pe, phi_ok, 4 * r)
                    split_product(PS[:, 0, 0:D], "R", "rwv").then_inc(rv_ps, 1)
                if M_:
                    wait(pe, ln_v["M"], 3 * m + 3)
                    wait(pe, xlo_ok["R"], s.before("F"))
                    wait(pe, phi_ok, 4 * s.before("R"))
                    transpose2(1, xn["M"]).then_inc(xT_ps["M"], 1)
                if P_:
                    wait(pe, qk_ok, p + 1)
                    split_product(PS[:, 7, 0:D], "P", "wvT").then_inc(v_ps, 1)
                if M_:
                    if s.static:
                        pe.wait_ge(tern, 11)
                    wait(pe, xT_ok["M"], m + 1)
                    wait(pe, xlo_ok["M"], m + 1)
                    wait(pe, phi_ok, 4 * s.before("R"))
                    for j in range(FC):
                        n = 0
                        for part in (xhi, xlo):
                            for c in range(KC):
                                last = pe.matmul(PS[:, 2 + j // 4, j % 4 * P:(j % 4 + 1) * P],
                                                 w1q[:, c, j * P:(j + 1) * P], part["M"][:, c, :],
                                                 start=(n == 0), stop=(n == 3))
                                n += 1
                    last.then_inc(m_ps, 1)
                if P_:
                    wait(pe, rope_ok, 3 * s.after("R"))
                    wait(pe, xT_ok["F"], s.after("F"))
                    wait(pe, xlo_ok["F"], s.after("F"))
                    wait(pe, hR_ok, s.before("R"))
                    features(4, 2).then_inc(tdk_ps, 1)
                if F_:
                    wait(pe, xT_ok["F"], f + 1)
                    wait(pe, xlo_ok["F"], f + 1)
                    wait(pe, v_ok, s.after("P"))
                    wait(pe, hF_ok, f)
                    split_product(PS[:, 7, :], "F", "fbT").then_inc(fh_ps, 1)
                if P_:
                    wait(pe, kmx_ok, p + 1)
                    wait(pe, hP_ok, 2 * p)
                    pe.transpose(PS[0:H, 6, 0:P], kmx[:, :], ident[:, :]).then_inc(kmxT_ps, 1)
                if R_:
                    wait(pe, rothi_ok, 3 * r + 3)
                    wait(pe, rotlo_ok, r + 1)
                    wait(pe, vlo_ok, r + 1)
                    wait(pe, xT_ok["M"], s.after("M"))
                    wait(pe, xlo_ok["M"], s.after("M"))
                    for base, bank in ((0, 0), (KEYS, 1)):
                        for c in range(HP):
                            last = pe.transpose(PS[:, bank, c * P // 2:(c + 1) * P // 2].bitcast(F16),
                                                split[:, base + c * P:base + (c + 1) * P], ident_h[:, :])
                    last.then_inc(rT_ps, 1)
                if F_:
                    wait(pe, kdiag_ok, 2 * s.after("P"))
                    wait(pe, hgT_ok, 2 * f)
                    split_product(PS[:, 6, 0:PROTO], "F", "protoT2", last_=False)
                    pe.matmul(PS[:, 6, 0:PROTO], ones[0:1, :], p2[0:1, :], start=False, stop=True)\
                        .then_inc(proto_ps, 1)
                if R_:
                    wait(pe, mh_ok, 2 * s.before("M") + (1 if M_ else 0))
                    masks((2, 3), mask_qk)
                if P_:
                    wait(pe, sq_ok, p + 1)
                    wait(pe, kdiag_ok, 2 * p + 2)
                    wait(pe, d2_ok, s.after("F"))
                    for c in range(KC):
                        pe.matmul(PS[:, 6, 0:H], sqT[:, 2 + c, :], half_sq[:, c, :], start=(c == 0), stop=False)
                    pe.matmul(PS[:, 6, 0:H], ones[0:H, :], kdiag[:, :], start=False, stop=True)
                    for c in range(KC):
                        last = pe.matmul(PS[:, 6, H:2 * H], sqT[:, c, :], half_sq[:, c, :],
                                         start=(c == 0), stop=(c == KC - 1))
                    last.then_inc(kb_ps, 1)
                if R_:
                    wait(pe, rqT_ok, r + 1)
                    wait(pe, rkT_ok, r + 1)
                    masks((0, 1), mask_qk)
                    for h in range(H):
                        o = SLOT * (h % 2)
                        last = pe.matmul(PS[:, h % 4, h // 4 * P:(h // 4 + 1) * P], rT[o:o + PARTS, h // 2, :],
                                         rT[o:o + PARTS, HP + h // 2, :], start=False, stop=True,
                                         skip_group_check=True)
                    last.then_inc(s1_ps, 1)
                if M_:
                    wait(pe, mlo_ok, m + 1)
                    wait(pe, kb_ok, s.after("P"))
                    wait(pe, d2_ok, s.after("F"))
                    for part in (mhi, mlo):
                        for j in range(FC):
                            last = pe.matmul(PS[:, 6, 0:D], part[:, j, :], w2q[:, j, :],
                                             start=(part is mhi and j == 0), stop=(part is mlo and j == FC - 1))
                    last.then_inc(y2_ps, 1)
                if P_:
                    wait(pe, kd_ok, p + 1)
                    features(4, 0).then_inc(tdq_ps, 1)
                if R_:
                    wait(pe, rmax_ok, r + 1)
                    pe.transpose(PS[0:H, 0, 0:P // 2].bitcast(F16), negmax[:, :], ident_h[:, :]).then_inc(nmT_ps, 1)
                    for j in (1, 2, 3, 0):
                        if j == 0:
                            wait(pe, nmT_ok, r + 1)
                        masks((j,), mask_kq)
                        for c in range(4):
                            h = 4 * c + j
                            o = SLOT * (h % 2)
                            pe.matmul(PS[:, j, c * P:(c + 1) * P], rT[o:o + PARTS, HP + h // 2, :],
                                      rT[o:o + PARTS, h // 2, :], start=False, stop=False, skip_group_check=True)
                    for h in range(H):
                        last = pe.matmul(PS[:, h % 4, h // 4 * P:(h // 4 + 1) * P], head_row[:, h, :], negmaxT[:, :],
                                         start=False, stop=True, skip_group_check=True)
                    last.then_inc(s2_ps, 1)
                if P_:
                    wait(pe, qe_ok, p + 1)
                    for j in range(HP):
                        last = pe.transpose(PS[0:MP, 4 + j // 4, j % 4 * P:(j % 4 + 1) * P],
                                            qe[:, j * MP:(j + 1) * MP], ident[:, :])
                    last.then_inc(qp_ps, 1)
                if F_:
                    wait(pe, hg_ok, f + 1)
                    for c in range(R2 // P):
                        last = pe.transpose(PS[:, 7, c * P:(c + 1) * P], hg[:, c * P:(c + 1) * P], ident[:, :])
                    last.then_inc(hgT_ps, 1)
                if P_:
                    wait(pe, kp_ok, p + 1)
                    wait(pe, v_ok, p + 1)
                    wait(pe, d2_ok, s.after("F"))
                    wait(pe, hgT_ok, 2 * s.before("F"))
                    wait(pe, out_ok, s.after("M"))
                    wait(pe, kb_ok, p + 1)
                    for j in range(HP):
                        last = pe.matmul(PS[0:MP, 6, 2 * VA * j:2 * VA * (j + 1)],
                                         kp[:, j * MP:(j + 1) * MP],
                                         va[:, 2 * j:2 * j + 2, :].rearrange("p h d -> p (h d)"), start=True, stop=True)
                    last.then_inc(ctx_ps, 1)
                if F_:
                    wait(pe, hgT_ok, 2 * f + 1)
                    for c in range(R2 // P):
                        pe.matmul(PS[:, 7, 0:D], hgT[:, c, :], faT[:, c, :], start=(c == 0), stop=False)
                    wait(pe, ctx_ok, s.after("P"))
                    wait(pe, out_ok, s.after("M"))
                    pe.transpose(PS[0:PROTO, 6, 0:P], hg[:, R2:], ident[:, :]).then_inc(hgT_ps, 1)
                if P_:
                    wait(pe, qp_ok, p + 1)
                    wait(pe, ctx_ok, p + 1)
                    for j in range(HP):
                        last = pe.matmul(PS[:, 4, 2 * VA * j:2 * VA * (j + 1)], qp[:, j, :], ctxt[:, j, :],
                                         start=True, stop=True)
                    last.then_inc(o_ps, 1)
                if F_:
                    wait(pe, hgT_ok, 2 * f + 2)
                    pe.matmul(PS[:, 7, 0:D], gT[:, :], fbias[:, :], start=False, stop=True).then_inc(y_ps, 1)
                if R_:
                    wait(pe, qp_ok, s.after("P"))
                    wait(pe, vlo_ok, r + 1)
                    for j in range(4):
                        wait(pe, plo_ok, 2 * r + 1 + j // 2)
                        for c in range(4):
                            h = 4 * c + j
                            o = PS[:, 5, VA * h:VA * (h + 1)]
                            pe.matmul(o, phi[:, j, c, :], vhi[:, h, :], start=True, stop=False)
                            pe.matmul(o, phi[:, j, c, :], vlo[:, h, :], start=False, stop=False)
                            last = pe.matmul(o, plo[:, j, c, :], vhi[:, h, :], start=False, stop=True)
                    last.then_inc(pv_ps, 1)
                if P_:
                    wait(pe, o_ok, 2 * p + 2)
                    wait(pe, phi_ok, 4 * s.after("R"))
                    wait(pe, xlo_ok["M"], s.after("M"))
                    wait(pe, xlo_ok["R"], s.before("F"))
                    transpose2(1, onorm).then_inc(oT_ps, 1)
                if E_:
                    wait(pe, ln_v["P"], 3 * e + 3)
                    wait(pe, phi_ok, 4 * s.after("R"))
                    transpose2(0, xn["P"]).then_inc(xT_ps["P"], 1)
                if R_:
                    wait(pe, ro_ok, 2 * r + 2)
                    wait(pe, o_ok, 2 * s.after("P"))
                    transpose2(4, rout).then_inc(roT_ps, 1)
                if P_:
                    wait(pe, oT_ok, p + 1)
                    wait(pe, ctx_ok, p + 1)
                    wait(pe, hgT_ok, 2 * s.after("F"))
                    token_major(PS[:, 6, 0:D], oT, wof).then_inc(of_ps, 1)
                if F_:
                    wait(pe, ln_v["R"], 3 * f + 3)
                    wait(pe, phi_ok, 4 * s.after("R"))
                    transpose2(1, xn["R"]).then_inc(xT_ps["R"], 1)
                if R_:
                    wait(pe, roT_ok, r + 1)
                    wait(pe, ro_ok, 2 * r + 2)
                    token_major(PS[:, 5, 0:D], roT, rwo).then_inc(wo_ps, 1)

            pe.wait_ge(g_const, 17)
            pe.wait_ge(load["P"], 16 * N_LOAD["P"])
            for i in range(KC):
                for c in range(KC):
                    last = pe.matmul(PS[:, 4 + i, 0:D], wo[:, c, i * P:(i + 1) * P], wfcT[:, c, :],
                                     start=(c == 0), stop=(c == KC - 1))
                last.then_inc(wof_ps, 1)
            for c in range(KC):
                last = pe.matmul(PS[:, 6, 0:D], bo[:, c:c + 1].to_broadcast([P, P]), wfcT[:, c, :],
                                 start=(c == 0), stop=(c == KC - 1))
            last.then_inc(wof_ps, 1)
            step(Step(-1))
            pe.wait_ge(wof_ok, 2)
            pe.wait_ge(s_const, 2)
            pe.wait_ge(wlo_ok, 2)
            step(Step(0))
            pe.wait_ge(p2_ok, 2)
            pe.wait_ge(hP_ok, 2)
            for c in range(KC):
                last = pe.matmul(PS[0:1, 6, 0:PROTO], ones[:, 0:1], proto_sq[:, c, :],
                                 start=(c == 0), stop=(c == KC - 1))
            last.then_inc(p2_ps, 1)
            pe.wait_ge(p2_ok, 8)
            pe.wait_ge(wlo_ok, 4)
            step(Step(1))
            pe.wait_ge(tern_abs, 14)
            pe.wait_ge(hP_ok, 4)
            pe.wait_ge(hgT_ok, 2)
            pe.wait_ge(wlo_ok, 6)
            pe.matmul(PS[:, 6, 0:2], ones[:, :], absum[:, :], start=True, stop=True).then_inc(tern_ps, 1)
            pe.wait_ge(tern, 1)
            for i in range(2, LOOP_FROM):
                step(Step(i))
            with pe.Fori(LOOP_FROM, LOOP_TO) as i:
                step(Step(i))
            for i in range(LOOP_TO, LAST_STEP + 1):
                step(Step(i))


def rotary_tables():
    inv = (np.float32(1.0) / np.power(np.float32(10000.0), np.arange(0, DH, 2, dtype=np.float32) / np.float32(DH)))
    theta = np.arange(P, dtype=np.float32)[:, None] * inv.astype(np.float32)[None, :]
    cos, sin = np.cos(theta).astype(np.float32), np.sin(theta).astype(np.float32)
    signed = np.stack([-sin, sin], axis=-1).reshape(P, DH)
    return np.tile(np.repeat(cos, 2, axis=-1), (1, 2 * H)), np.tile(signed, (1, 2 * H))


def kernel(**inputs):
    import concourse.bacc as _bacc
    from concourse.bass_utils import run_bass_kernel_spmd as _run

    a = {k: np.asarray(x) for k, x in inputs.items()}

    def cols(x, n):
        return x.reshape(n, P).T

    cos, sin = rotary_tables()
    laid = {
        "ids": np.stack([a["x"].T, a["itok_BS_0_511"].T, a["mask_BS_i1_0"].T], axis=1),
        "word": a["L0_tok_word_emb"], "pos": a["L0_tok_pos_emb"], "type": a["L0_tok_type_emb"],
        "gamma": a["L0_tok_ln_gamma"], "beta": a["L0_tok_ln_beta"],
        "wqkT": np.concatenate([a["L0_attn_Wq"].T, a["L0_attn_Wk"].T], axis=1), "wvT": a["L0_attn_Wv"].T,
        "wo": a["L0_attn_Wo"], "wfcT": a["L0_attn_Wfc"].T,
        "bqk": cols(np.concatenate([a["L0_attn_bq"], a["L0_attn_bk"]]), 4), "bv": a["L0_attn_bv"],
        "bo": cols(a["L0_attn_bo"], KC), "bfc": a["L0_attn_bfc"], "projT": a["L0_attn_proj"].T,
        "protoT": a["L0_ffn_prototypes"].T, "fbT": a["L0_ffn_B"].reshape(R2, D).T,
        "faT": a["L0_ffn_A"].transpose(0, 2, 1).reshape(R2, D), "fbias": a["L0_ffn_bias"],
        "temp": a["L0_ffn_temp"].reshape(1),
        "rwqk": np.concatenate([a["L1_attn_Wq"], a["L1_attn_Wk"]], axis=1), "rwv": a["L1_attn_Wv"],
        "rwo": a["L1_attn_Wo"], "rope_cos": cos, "rope_sin": sin,
        "w1T": a["L1_ffn_W1"].T, "w2T": a["L1_ffn_W2"].T, "b1": cols(a["L1_ffn_b1"], FC), "b2": a["L1_ffn_b2"],
    }
    nc = _bacc.Bacc("TRN2", target_bir_lowering=False, num_devices=1)
    arrays, aps = {}, {}
    for name, x in laid.items():
        x = np.ascontiguousarray(x)
        arrays[f"in_{name}"] = x
        aps[name] = nc.dram_tensor(f"in_{name}", x.shape, mybir.dt.from_np(x.dtype), kind="ExternalInput").ap()
    out = nc.dram_tensor("out_0", (TILES, P, D), F32, kind="ExternalOutput").ap()
    program(nc, aps, out)
    r = _run(nc, [arrays], core_ids=[0])
    return r.results[0]["out_0"]
```
